# Optimizing a Trainium2 kernel written in Bass

```python
import numpy as np
import jax
import jax.numpy as jnp

def _softmax(x, axis=-1):
    return jax.nn.softmax(x, axis=axis)

def _gelu(x):
    return jax.nn.gelu(x, approximate=True)

def _silu(x):
    return jax.nn.silu(x)

def _sigmoid(x):
    return jax.nn.sigmoid(x)

def _layernorm(x, axis=-1, eps=1e-05):
    m = jnp.mean(x, axis=axis, keepdims=True)
    v = jnp.var(x, axis=axis, keepdims=True)
    return (x - m) / jnp.sqrt(v + eps)

def _scatter_add(tgt, idx, src, axis=0):
    return tgt.at[idx].add(src)

def _segment_sum(src, seg, n):
    return jax.ops.segment_sum(src, seg, n)
kernel_name = 'mk_lm_tower_d1_tok_ids1024_r4_6319af'

def setup_inputs(seed: int=0):
    np.random.seed(seed)
    _w = jnp.asarray

    def _rec_inputs():
        import jax
        import jax.numpy as jnp
        _rk = jax.random.key(seed)
        x = jax.random.randint(jax.random.fold_in(_rk, 1), (16, 512), 0, 12564, jnp.int32)
        return x
    x = _rec_inputs()

    def _L0_tok_setup():
        import jax, jax.numpy as jnp
        import numpy as np
        VOCAB = 50257
        NUM_DIM = 256
        BATCH = 4
        SEQ = 1024
        key = jax.random.key(seed)
        k_tok, k_w, k_b = jax.random.split(key, 3)
        tokens = jax.random.randint(k_tok, (BATCH, SEQ), 0, VOCAB)
        weight = jax.random.normal(k_w, (NUM_DIM, VOCAB), dtype=jnp.float32) * 0.02
        bias = jax.random.normal(k_b, (NUM_DIM,), dtype=jnp.float32) * 0.02
        return {'tokens': tokens, 'weight': weight, 'bias': bias}
    _L0_tok_all = _L0_tok_setup()
    _L0_tok_in = {k: v for k, v in _L0_tok_all.items() if k in ('weight', 'bias')}
    del _L0_tok_all

    def _L0_attn_setup():
        import jax, jax.numpy as jnp
        import numpy as np
        H = 16
        EPS = 1e-12

        def _l2norm(t):
            n = jnp.sqrt(jnp.sum(t * t, axis=-1, keepdims=True))
            return t / jnp.maximum(n, EPS)
        key = jax.random.key(seed)
        ks = jax.random.split(key, 7)
        B, L, D = (2, 512, 256)
        s = 0.02
        return {'x': jax.random.normal(ks[0], (B, L, D), dtype=jnp.float32), 'Wq': jax.random.normal(ks[1], (D, D), dtype=jnp.float32) * s, 'Wk': jax.random.normal(ks[2], (D, D), dtype=jnp.float32) * s, 'Wv': jax.random.normal(ks[3], (D, D), dtype=jnp.float32) * s, 'Wo': jax.random.normal(ks[4], (D, D), dtype=jnp.float32) * s, 'Wb': jax.random.normal(ks[5], (D, H), dtype=jnp.float32) * s, 'bb': jnp.zeros((H,), dtype=jnp.float32)}
    _L0_attn_all = _L0_attn_setup()
    _L0_attn_in = {k: v for k, v in _L0_attn_all.items() if k in ('Wq', 'Wk', 'Wv', 'Wo', 'Wb', 'bb')}
    del _L0_attn_all

    def _L0_ffn_setup():
        import jax, jax.numpy as jnp
        import numpy as np
        B, S, D = (8, 1024, 256)
        E, R, K = (6, 16, 2)
        key = jax.random.key(seed)
        ks = jax.random.split(key, 9)
        sc = 0.02
        return {'x': jax.random.normal(ks[0], (B, S, D), jnp.float32), 'base_W': jax.random.normal(ks[1], (D, D), jnp.float32) * sc, 'base_b': jax.random.normal(ks[2], (D,), jnp.float32) * sc, 'shared_A': jax.random.normal(ks[3], (R, D), jnp.float32) * sc, 'shared_B': jax.random.normal(ks[4], (D, R), jnp.float32) * sc, 'routed_A': jax.random.normal(ks[5], (E, R, D), jnp.float32) * sc, 'routed_B': jax.random.normal(ks[6], (E, D, R), jnp.float32) * sc, 'router_W': jax.random.normal(ks[7], (E, D), jnp.float32) * sc, 'router_b': jax.random.normal(ks[8], (E,), jnp.float32) * sc}
    _L0_ffn_all = _L0_ffn_setup()
    _L0_ffn_in = {k: v for k, v in _L0_ffn_all.items() if k in ('base_W', 'base_b', 'shared_A', 'shared_B', 'routed_A', 'routed_B', 'router_W', 'router_b')}
    del _L0_ffn_all
    return {'x': x, 'L0_tok_weight': _L0_tok_in['weight'], 'L0_tok_bias': _L0_tok_in['bias'], 'L0_attn_Wq': _L0_attn_in['Wq'], 'L0_attn_Wk': _L0_attn_in['Wk'], 'L0_attn_Wv': _L0_attn_in['Wv'], 'L0_attn_Wo': _L0_attn_in['Wo'], 'L0_attn_Wb': _L0_attn_in['Wb'], 'L0_attn_bb': _L0_attn_in['bb'], 'L0_ffn_base_W': _L0_ffn_in['base_W'], 'L0_ffn_base_b': _L0_ffn_in['base_b'], 'L0_ffn_shared_A': _L0_ffn_in['shared_A'], 'L0_ffn_shared_B': _L0_ffn_in['shared_B'], 'L0_ffn_routed_A': _L0_ffn_in['routed_A'], 'L0_ffn_routed_B': _L0_ffn_in['routed_B'], 'L0_ffn_router_W': _L0_ffn_in['router_W'], 'L0_ffn_router_b': _L0_ffn_in['router_b']}

def reference(x, L0_tok_weight, L0_tok_bias, L0_attn_Wq, L0_attn_Wk, L0_attn_Wv, L0_attn_Wo, L0_attn_Wb, L0_attn_bb, L0_ffn_base_W, L0_ffn_base_b, L0_ffn_shared_A, L0_ffn_shared_B, L0_ffn_routed_A, L0_ffn_routed_B, L0_ffn_router_W, L0_ffn_router_b):
    import jax
    import jax.numpy as jnp

    def _L0_tok_ref(tokens, weight, bias):
        import jax, jax.numpy as jnp
        import numpy as np
        VOCAB = 50257
        NUM_DIM = 256
        BATCH = 4
        SEQ = 1024
        table = weight.T
        return jnp.take(table, tokens, axis=0) + bias

    def _L0_attn_ref(x, Wq, Wk, Wv, Wo, Wb, bb):
        import jax, jax.numpy as jnp
        import numpy as np
        H = 16
        EPS = 1e-12

        def _l2norm(t):
            n = jnp.sqrt(jnp.sum(t * t, axis=-1, keepdims=True))
            return t / jnp.maximum(n, EPS)
        B, L, Dm = x.shape
        Dh = Dm // H
        q = (x @ Wq).reshape(B, L, H, Dh)
        k = (x @ Wk).reshape(B, L, H, Dh)
        v = (x @ Wv).reshape(B, L, H, Dh)
        beta = jax.nn.sigmoid(x @ Wb + bb)
        q = _l2norm(q)
        k = _l2norm(k)
        scores = jnp.einsum('blhd,bthd->bhlt', q, k)
        scores = scores * beta.transpose(0, 2, 1)[:, :, None, :]
        mask = jnp.tril(jnp.ones((L, L), dtype=scores.dtype))
        scores = scores * mask
        out = jnp.einsum('bhlt,bthe->blhe', scores, v).reshape(B, L, Dm)
        return out @ Wo

    def _L0_ffn_ref(x, base_W, base_b, shared_A, shared_B, routed_A, routed_B, router_W, router_b):
        import jax, jax.numpy as jnp
        import numpy as np
        B, S, D = (8, 1024, 256)
        E, R, K = (6, 16, 2)
        base_out = jax.lax.stop_gradient(jnp.einsum('bsi,oi->bso', x, base_W) + base_b)
        shared_out = jnp.einsum('bsr,or->bso', jnp.einsum('bsi,ri->bsr', x, shared_A), shared_B)
        logits = jnp.einsum('bsi,ei->bse', x, router_W) + router_b
        gate = jax.nn.softmax(logits, axis=-1)
        topk_w, topk_i = jax.lax.top_k(gate, K)
        sparse_w = jnp.sum(jax.nn.one_hot(topk_i, E, dtype=gate.dtype) * topk_w[..., None], axis=-2)
        sparse_w = sparse_w / (jnp.sum(sparse_w, axis=-1, keepdims=True) + 1e-06)
        h = jnp.einsum('bsi,eri->bser', x, routed_A)
        routed_outs = jnp.einsum('bser,eor->bseo', h, routed_B)
        routed_out = jnp.einsum('bseo,bse->bso', routed_outs, sparse_w)
        return base_out + shared_out + routed_out
    h = _L0_tok_ref(x, L0_tok_weight, L0_tok_bias)
    h = h + _L0_attn_ref(_layernorm(h, axis=-1), L0_attn_Wq, L0_attn_Wk, L0_attn_Wv, L0_attn_Wo, L0_attn_Wb, L0_attn_bb)
    h = h + _L0_ffn_ref(_layernorm(h, axis=-1), L0_ffn_base_W, L0_ffn_base_b, L0_ffn_shared_A, L0_ffn_shared_B, L0_ffn_routed_A, L0_ffn_routed_B, L0_ffn_router_W, L0_ffn_router_b)
    return h

_drawn_inputs = setup_inputs


def setup_inputs(seed=0):
    import zlib

    import numpy as np

    out = dict(_drawn_inputs(seed))
    spreads = {'L0_attn_bb': (0.0, 0.1)}
    factors = {'L0_ffn_base_b': 5.886,
     'L0_ffn_shared_A': 4.305,
     'L0_ffn_shared_B': 3.906,
     'L0_ffn_routed_A': 6.566,
     'L0_ffn_routed_B': 6.297,
     'L0_ffn_router_W': 8.0,
     'L0_ffn_router_b': 8.0}
    for name, (base, spread) in spreads.items():
        noise = np.random.default_rng([zlib.crc32(name.encode()), seed]).standard_normal(out[name].shape)
        drawn = base * np.exp(spread * noise) if base else spread * noise
        out[name] = jnp.asarray(drawn.astype(out[name].dtype))
    for name, factor in factors.items():
        out[name] = (out[name] * factor).astype(out[name].dtype)
    return out
```

```python
import numpy as np

import concourse.bass as bass
from concourse import mybir

F32 = mybir.dt.float32
U32 = mybir.dt.uint32
ALU = mybir.AluOpType
ACT = mybir.ActivationFunctionType
AX = mybir.AxisListType

P = 128
SEQS = 16
L = 512
T = L // P
D = 256
KH = D // P
H = 16
DH = D // H
HM = H // KH
PAIRS = H // 2
UNITS = 4
UH = H // UNITS
E = 6
R = 16
AR = E * R + R
NR = AR + E
BR = AR + 1
VZ = 48
EPS_LN = 1e-5
EPS_NORM2 = 1e-12 ** 2
LN_SCALE = 65536.0
ROOT_SCALE = 256.0
RANK_EPS = 1e-6

FRONT = ["x0", "x1", "q0", "q1", "k0", "k1", "v0", "v1", "n0", "v2", "v3", "n1", "t0", "t1", "t2", "t3"]
FRONT_ACT = [u for u in FRONT if u[0] != "n"]
NF, NFA = len(FRONT), len(FRONT_ACT)
LN_STEPS = 2
GATE_STEPS = 12
KNORM_STEPS = 3
QEXP_DMAS = HM


class Seq:

    def __init__(self, j, offset):
        self.number = j * 2 + offset
        self.parity = offset % 2
        self.half = j + offset // 2

    def at(self, per_sequence, k):
        return self.number * per_sequence + k

    def at_half(self, per_sequence, k):
        return self.half * per_sequence + k


def wait_for(engine, semaphore, value):
    if isinstance(value, int) and value <= 0:
        return
    engine.wait_ge(semaphore, value)


def stand(engine, semaphore):
    engine.sem_inc(semaphore, 1)


def v_heads(buffer, t, pair, n):
    x = buffer[:, t, pair:pair + n, :].rearrange("p g (three d) -> p g three d", d=DH)
    return x[:, :, 0:3:2, :]


def steps(engine, run):
    def seqs(j, s):
        return Seq(j, s + 1), Seq(j, s), Seq(j, s - 1)

    a, b, c = seqs(0, -1)
    run(a, None, None)
    a, b, c = seqs(0, 0)
    run(a, b, None)
    run(*seqs(0, 1))
    with engine.Fori(0, (SEQS - 4) // 2) as j:
        run(*seqs(j, 2))
        run(*seqs(j, 3))
    run(*seqs(0, SEQS - 2))
    a, b, c = seqs(0, SEQS - 1)
    run(None, b, c)
    a, b, c = seqs(0, SEQS)
    run(None, None, c)


def build(nc, tokens, table, tok_bias, w_q, w_k, w_vb, bb, w_o, w_base, w_ar, w_b, router_b,
          ident_in, causal_in, headmask_in, order_in, out):
    from contextlib import ExitStack

    with ExitStack() as ctx:
        def sb(name, shape, dt=F32):
            return ctx.enter_context(nc.sbuf_tensor(name, shape, dt))

        def ps(name, shape):
            return ctx.enter_context(nc.psum_tensor(name, shape, F32))

        def sem(name):
            return ctx.enter_context(nc.semaphore(name))

        idx_all = sb("idx_all", [P, SEQS * T], U32)
        bias_tok = sb("bias_tok", [P, D])
        wq = sb("wq", [P, KH, D])
        wk = sb("wk", [P, KH, D])
        wvb = sb("wvb", [P, KH, D + H])
        bbeta = sb("bbeta", [P, H])
        wo = sb("wo", [P, KH, D])
        wbase = sb("wbase", [P, KH, D])
        war = sb("war", [P, KH, NR])
        wb = sb("wb", [BR, D])
        brouter = sb("brouter", [P, E])
        ident = sb("ident", [P, P])
        causal = sb("causal", [P, P])
        headmask = sb("headmask", [P, P])
        order = sb("order", [P, 2, E, E])
        eps_ln = sb("eps_ln", [P, 1])
        idx = sb("idx", [P, T], U32)
        rows = sb("rows", [P, T, D])
        h = [sb(f"h{i}", [P, T, D]) for i in range(2)]
        st1 = sb("st1", [P, T, 6])
        mv1 = sb("mv1", [P, T, 2])
        lnv1 = sb("lnv1", [P, T])
        rstd1 = sb("rstd1", [P, T])
        nmr1 = sb("nmr1", [P, T])
        xn = sb("xn", [P, T, D])
        xT = sb("xT", [P, KH, L])
        qT = [sb(f"qT{i}", [P, KH, L]) for i in range(2)]
        kT = [sb(f"kT{i}", [P, KH, L]) for i in range(2)]
        qexp = [sb(f"qexp{i}", [P, KH, HM, L]) for i in range(2)]
        qsq = sb("qsq", [P, KH, L])
        qn2 = sb("qn2", [P, KH, L])
        rq = [sb(f"rq{i}", [P, KH, L]) for i in range(2)]
        vraw = sb("vraw", [P, T, D + H])
        ktok = [sb(f"ktok{i}", [P, T, D]) for i in range(2)]
        ksq = sb("ksq", [P, T, D])
        kn2 = sb("kn2", [P, T, H])
        kn2c = sb("kn2c", [P, T, H])
        kln = sb("kln", [P, T, H])
        rk = sb("rk", [P, T, H])
        zb = sb("zb", [P, T, H])
        ez = sb("ez", [P, T, H])
        ez1 = sb("ez1", [P, T, H])
        beta = sb("beta", [P, T, H])
        vscale = sb("vscale", [P, T, H])
        vz = [sb(f"vz{i}", [P, T, PAIRS, VZ]) for i in range(2)]
        probs = [sb(f"probs{i}", [P, UNITS, UH, P]) for i in range(2)]
        state = sb("state", [P, KH, P])
        attnT = [sb(f"attnT{i}", [P, KH, P]) for i in range(2)]
        h2 = [sb(f"h2_{i}", [P, T, D]) for i in range(2)]
        st2 = sb("st2", [P, T, 6])
        mv2 = sb("mv2", [P, T, 2])
        lnv2 = sb("lnv2", [P, T])
        rstd2 = sb("rstd2", [P, T])
        nmr2 = sb("nmr2", [P, T])
        yn = sb("yn", [P, T, D])
        yT = sb("yT", [P, KH, L])
        logit = sb("logit", [P, T, E])
        lmax = sb("lmax", [P, T])
        lsub = sb("lsub", [P, T, E])
        elog = sb("elog", [P, T, E])
        above = sb("above", [P, T, 2, E, E])
        rank = sb("rank", [P, T, E])
        esel = sb("esel", [P, T, E])
        esum = sb("esum", [P, T])
        eall = sb("eall", [P, T])
        gden = sb("gden", [P, T])
        ginv = sb("ginv", [P, T])
        gate = sb("gate", [P, T, E + 1])
        aw = sb("aw", [P, T, BR])
        awT = sb("awT", [BR, L])
        outb = sb("outb", [P, T, D])

        front = [ps(f"front{i}", [P, L]) for i in range(2)]
        score = [ps(f"score{i}", [P, UH, P]) for i in range(2)]
        oT = ps("oT", [P, 2, KH, P])
        kv = ps("kv", [P, KH, P])
        tok = ps("tok", [P, 2, D])
        cps = ps("cps", [P, L])

        loaded = sem("loaded")
        idx_loaded = sem("idx_loaded")
        gathered = sem("gathered")
        qexp_landed = [sem(f"qexp_landed{i}") for i in range(2)]
        stored = sem("stored")
        pool_set = sem("pool_set")
        idx_copied = sem("idx_copied")
        pool_stood = sem("pool_stood")
        h_ready = sem("h_ready")
        xn_ready = sem("xn_ready")
        yn_ready = sem("yn_ready")
        vz_ready = sem("vz_ready")
        front_ready = sem("front_ready")
        scored = sem("scored")
        oT_ready = sem("oT_ready")
        kv_ready = sem("kv_ready")
        wo_ready = sem("wo_ready")
        cps_ready = sem("cps_ready")
        ffn_ready = sem("ffn_ready")
        front_out = sem("front_out")
        qsq_ready = sem("qsq_ready")
        ln1_done = sem("ln1_done")
        rstd1_ready = sem("rstd1_ready")
        qln_done = sem("qln_done")
        rq_ready = sem("rq_ready")
        ez_ready = sem("ez_ready")
        kln_done = sem("kln_done")
        rk_ready = sem("rk_ready")
        ln2_done = sem("ln2_done")
        rstd2_ready = sem("rstd2_ready")
        cps_out = sem("cps_out")
        elog_ready = sem("elog_ready")
        vec_set = sem("vec_set")
        stats1 = sem("stats1")
        var1_ready = sem("var1_ready")
        nmr1_ready = sem("nmr1_ready")
        qn2_ready = sem("qn2_ready")
        knorm = sem("knorm")
        kn2_done = sem("kn2_done")
        beta_steps = sem("beta_steps")
        masked = sem("masked")
        attn_ready = sem("attn_ready")
        state_ready = sem("state_ready")
        h2_ready = sem("h2_ready")
        stats2 = sem("stats2")
        var2_ready = sem("var2_ready")
        nmr2_ready = sem("nmr2_ready")
        gating = sem("gating")
        out_ready = sem("out_ready")
        vec_stood = sem("vec_stood")

        out_t = out.rearrange("(s t p) d -> s p t d", s=SEQS, t=T)

        loads = [(bias_tok[:], tok_bias.partition_broadcast(P)), (ident[:], ident_in),
                 (wq[:], w_q.rearrange("(k p) m -> p k m", p=P)), (wk[:], w_k.rearrange("(k p) m -> p k m", p=P)),
                 (wvb[:], w_vb.rearrange("(k p) m -> p k m", p=P)), (causal[:], causal_in),
                 (headmask[:], headmask_in), (bbeta[:], bb.partition_broadcast(P)),
                 (wo[:], w_o.rearrange("(k p) m -> p k m", p=P)),
                 (wbase[:], w_base.rearrange("(k p) m -> p k m", p=P)),
                 (war[:], w_ar.rearrange("(k p) m -> p k m", p=P)), (wb[:], w_b),
                 (brouter[:], router_b.partition_broadcast(P)),
                 (order[:].rearrange("p a i j -> p (a i j)"), order_in.partition_broadcast(P))]
        LOADED = 16 * len(loads)

        with nc.Block() as block:
            @block.sync
            def _(sp):
                sp.dma_start(idx_all[:], tokens).then_inc(idx_loaded, 16)
                for dst, src in loads:
                    sp.dma_start(dst, src).then_inc(loaded, 16)
                wait_for(sp, pool_set, 1)
                wait_for(sp, vec_set, 1)

                def run(a, b, c):
                    if a:
                        wait_for(sp, front_out, a.at(NFA, FRONT_ACT.index("q1") + 1))
                        wait_for(sp, scored, a.at(T * UNITS, -T * UNITS))
                        for i in range(HM):
                            r = slice(DH * i, DH * i + DH)
                            sp.dma_start(qexp[a.parity][r, :, i, :], qT[a.parity][r, :, :]) \
                              .then_inc(qexp_landed[a.parity], 16)
                    if c:
                        wait_for(sp, out_ready, c.at(T, T))
                        sp.dma_start(out_t[c.number], outb[:]).then_inc(stored, 16)

                steps(sp, run)
                sp.wait_ge(stored, 16 * SEQS)

            @block.gpsimd
            def _(pool):
                def gather(n):
                    nc.gpsimd.tensor_copy(idx[:], idx_all[:, bass.ds(n * T, T)]).then_inc(idx_copied, 1)
                    pool.wait_ge(idx_copied, n + 1)
                    stand(pool, pool_stood)
                    for t in range(T):
                        nc.gpsimd.indirect_dma_start(
                            out=rows[:, t, :], out_offset=None, in_=table,
                            in_offset=bass.IndirectOffsetOnAxis(ap=idx[:, t:t + 1], axis=0),
                        ).then_inc(gathered, 16)

                pool.wait_ge(idx_loaded, 16)
                gather(0)
                nc.gpsimd.memset(vz[0][:], 0.0)
                nc.gpsimd.memset(vz[1][:], 0.0)
                nc.gpsimd.memset(gate[:], 1.0)
                nc.gpsimd.memset(aw[:], 1.0)
                nc.gpsimd.memset(qexp[0][:], 0.0).then_inc(pool_set, 1)
                pool.wait_ge(pool_set, 1)
                pool.wait_ge(loaded, LOADED)

                def run(a, b, c):
                    if c:
                        wait_for(pool, nmr2_ready, c.at(1, 1))
                        wait_for(pool, cps_ready, c.at(4, -2))
                        stand(pool, pool_stood)
                        for t in range(T):
                            nc.gpsimd.tensor_scalar(yn[:, t, :], h2[c.parity][:, t, :], rstd2[:, t:t + 1],
                                                    nmr2[:, t:t + 1], ALU.mult, ALU.add).then_inc(yn_ready, 1)
                    if not a:
                        return
                    pool.wait_ge(gathered, a.at(16 * T, 16 * T))
                    for t in range(T):
                        wait_for(pool, h2_ready, a.at(T, -2 * T + t + 1))
                        nc.gpsimd.tensor_tensor(h[a.parity][:, t, :], rows[:, t, :], bias_tok[:],
                                                ALU.add).then_inc(h_ready, 1)
                    pool.wait_ge(nmr1_ready, a.at(1, 1))
                    wait_for(pool, front_ready, a.at(NF, FRONT.index("x1") + 1 - NF))
                    stand(pool, pool_stood)
                    for t in range(T):
                        nc.gpsimd.tensor_scalar(xn[:, t, :], h[a.parity][:, t, :], rstd1[:, t:t + 1],
                                                nmr1[:, t:t + 1], ALU.mult, ALU.add).then_inc(xn_ready, 1)
                    pool.wait_ge(h_ready, a.at(T, T))
                    if not (isinstance(a.number, int) and a.number + 1 == SEQS):
                        gather(a.number + 1)
                    pool.wait_ge(knorm, a.at(KNORM_STEPS, KNORM_STEPS))
                    wait_for(pool, oT_ready, a.at(T, -T))
                    for t in range(T):
                        v3 = vraw[:, t, 0:D].rearrange("p (g two d) -> p g two d", two=2, d=DH)
                        s3 = vscale[:, t, :].rearrange("p (g two) -> p g two", two=2).unsqueeze(3) \
                            .broadcast_to([P, PAIRS, 2, DH])
                        nc.gpsimd.tensor_tensor(v_heads(vz[a.parity], t, 0, PAIRS), v3, s3, ALU.mult) \
                            .then_inc(vz_ready, 1)

                steps(pool, run)

            @block.scalar
            def _(act):
                act.wait_ge(vec_set, 1)

                def out_of(a, name, dst, src):
                    nc.scalar.activation(dst, src, ACT.Copy).then_inc(front_out, 1)

                def ready(a, name):
                    act.wait_ge(front_ready, a.at(NF, FRONT.index(name) + 1))
                    return front[FRONT.index(name) % 2]

                def norm_q(a, m):
                    act.wait_ge(qn2_ready, a.at(KH, m + 1))
                    nc.scalar.activation(qn2[:, m, :], qn2[:, m, :], ACT.Ln, scale=LN_SCALE).then_inc(qln_done, 1)
                    act.wait_ge(qln_done, a.at(KH, m + 1))
                    nc.scalar.activation(rq[a.parity][:, m, :], qn2[:, m, :], ACT.Exp, scale=-0.5) \
                        .then_inc(rq_ready, 1)

                def take_v(a, t):
                    src = ready(a, f"v{t}")
                    wait_for(act, vz_ready, a.at(T, t + 1 - T))
                    out_of(a, f"v{t}", vraw[:, t, :], src[:, 0:D + H])

                def take_k(a, t):
                    src = ready(a, f"t{t}")
                    nc.scalar.activation(ksq[:, t, :], src[:, 0:D], ACT.Square)
                    out_of(a, f"t{t}", ktok[a.parity][:, t, :], src[:, 0:D])

                def run(a, b, c):
                    if c:
                        act.wait_ge(cps_ready, c.at(4, 1))
                        nc.scalar.activation(yT[:, 0, :], cps[:], ACT.Copy).then_inc(cps_out, 1)
                    if a:
                        act.wait_ge(var1_ready, a.at(1, 1))
                        nc.scalar.activation(lnv1[:], mv1[:, :, 1], ACT.Ln, bias=eps_ln[:, 0:1]).then_inc(ln1_done, 1)
                        act.wait_ge(ln1_done, a.at(1, 1))
                        wait_for(act, xn_ready, a.at(T, 0))
                        nc.scalar.activation(rstd1[:], lnv1[:], ACT.Exp, scale=-0.5).then_inc(rstd1_ready, 1)
                    if c:
                        act.wait_ge(cps_ready, c.at(4, 2))
                        nc.scalar.activation(yT[:, 1, :], cps[:], ACT.Copy).then_inc(cps_out, 1)
                    if a:
                        for k in range(KH):
                            out_of(a, f"x{k}", xT[:, k, :], ready(a, f"x{k}")[:])
                        for m in range(KH):
                            src = ready(a, f"q{m}")
                            nc.scalar.activation(qsq[:, m, :], src[:], ACT.Square).then_inc(qsq_ready, 1)
                            out_of(a, f"q{m}", qT[a.parity][:, m, :], src[:])
                        for m in range(KH):
                            out_of(a, f"k{m}", kT[a.parity][:, m, :], ready(a, f"k{m}")[:])
                        take_v(a, 0)
                        take_v(a, 1)
                    if c:
                        act.wait_ge(gating, c.at(GATE_STEPS, 3))
                        nc.scalar.activation(elog[:], lsub[:], ACT.Exp).then_inc(elog_ready, 1)
                    if a:
                        norm_q(a, 0)
                        take_v(a, 2)
                        take_v(a, 3)
                        norm_q(a, 1)
                        take_k(a, 0)
                        take_k(a, 1)
                    if c:
                        act.wait_ge(cps_ready, c.at(4, 4))
                        nc.scalar.activation(awT[:], cps[0:BR, :], ACT.Copy).then_inc(cps_out, 1)
                    if a:
                        take_k(a, 2)
                        take_k(a, 3)
                        act.wait_ge(knorm, a.at(KNORM_STEPS, 1))
                        nc.scalar.activation(ez[:], zb[:], ACT.Exp, scale=-1.0).then_inc(ez_ready, 1)
                        act.wait_ge(knorm, a.at(KNORM_STEPS, 2))
                        nc.scalar.activation(kln[:], kn2c[:], ACT.Ln, scale=LN_SCALE).then_inc(kln_done, 1)
                        act.wait_ge(kln_done, a.at(1, 1))
                        nc.scalar.activation(rk[:], kln[:], ACT.Exp, scale=-0.5).then_inc(rk_ready, 1)
                    if b:
                        act.wait_ge(var2_ready, b.at(1, 1))
                        nc.scalar.activation(lnv2[:], mv2[:, :, 1], ACT.Ln, bias=eps_ln[:, 0:1]).then_inc(ln2_done, 1)
                        act.wait_ge(ln2_done, b.at(1, 1))
                        nc.scalar.activation(rstd2[:], lnv2[:], ACT.Exp, scale=-0.5).then_inc(rstd2_ready, 1)

                steps(act, run)

            @block.vector
            def _(dve):
                nc.vector.memset(eps_ln[:], EPS_LN)
                nc.vector.memset(qexp[1][:], 0.0).then_inc(vec_set, 1)
                dve.wait_ge(vec_set, 1)
                dve.wait_ge(loaded, LOADED)
                dve.wait_ge(pool_set, 1)

                def mask(b, t, m):
                    for u in (2 * m, 2 * m + 1):
                        dve.wait_ge(scored, b.at(T * UNITS, UNITS * t + u + 1))
                        if u == 0:
                            wait_for(dve, oT_ready, b.at(T, t - 1))
                        nc.vector.tensor_tensor(
                            probs[t % 2][:, u, :, :], score[u % 2][:],
                            causal[:].unsqueeze(1).broadcast_to([P, UH, P]), ALU.mult).then_inc(masked, 1)

                def attn_out(b, t):
                    dve.wait_ge(oT_ready, b.at(T, t + 1))
                    wait_for(dve, wo_ready, b.at(T, t - 1))
                    if t == 0:
                        dve.wait_ge(rq_ready, b.at(KH, KH))
                    nc.vector.scalar_tensor_tensor(
                        attnT[t % 2][:], oT[:, t % 2, :, :], ROOT_SCALE, rq[b.parity][:, :, t * P:t * P + P],
                        ALU.mult, ALU.mult).then_inc(attn_ready, 1)

                def state_out(b, t):
                    dve.wait_ge(kv_ready, b.at(T - 1, t + 1))
                    nc.vector.tensor_tensor(state[:], kv[:], headmask[:].unsqueeze(1).broadcast_to([P, KH, P]),
                                            ALU.mult).then_inc(state_ready, 1)

                def residual1(b, t):
                    dve.wait_ge(wo_ready, b.at(T, t + 1))
                    nc.vector.tensor_tensor(h2[b.parity][:, t, :], tok[:, 0, :], h[b.parity][:, t, :],
                                            ALU.add).then_inc(h2_ready, 1)
                    dve.wait_ge(h2_ready, b.at(T, t + 1))
                    nc.vector.bn_stats(st2[:, t, :], h2[b.parity][:, t, :]).then_inc(stats2, 1)

                def residual2(c, t):
                    dve.wait_ge(ffn_ready, c.at(T, t + 1))
                    if t == 0:
                        wait_for(dve, stored, c.at(16, 0))
                    nc.vector.tensor_tensor(outb[:, t, :], tok[:, 1, :], h2[c.parity][:, t, :],
                                            ALU.add).then_inc(out_ready, 1)

                def clamp_q(a, m):
                    name = f"n{m}"
                    dve.wait_ge(front_ready, a.at(NF, FRONT.index(name) + 1))
                    nc.vector.tensor_scalar(qn2[:, m, :], front[FRONT.index(name) % 2][:], EPS_NORM2, None,
                                            ALU.max).then_inc(qn2_ready, 1)

                def gate_a(c):
                    dve.wait_ge(cps_ready, c.at(4, 3))
                    r = cps[:, 0:T * NR].rearrange("p (t n) -> p t n", n=NR)
                    nc.vector.tensor_tensor(logit[:], r[:, :, AR:NR], brouter[:].unsqueeze(1).broadcast_to([P, T, E]),
                                            ALU.add).then_inc(gating, 1)
                    dve.wait_ge(gating, c.at(GATE_STEPS, 1))
                    nc.vector.tensor_reduce(lmax[:], logit[:], AX.X, ALU.max).then_inc(gating, 1)
                    dve.wait_ge(gating, c.at(GATE_STEPS, 2))
                    nc.vector.tensor_tensor(lsub[:], logit[:], lmax[:].unsqueeze(2).broadcast_to([P, T, E]),
                                            ALU.subtract).then_inc(gating, 1)
                    for n, op in enumerate((ALU.is_gt, ALU.is_ge)):
                        for t in range(T):
                            last = nc.vector.tensor_tensor(
                                above[:, t, n, :, :], logit[:, t, :].unsqueeze(1).broadcast_to([P, E, E]),
                                logit[:, t, :].unsqueeze(2).broadcast_to([P, E, E]), op)
                    last.then_inc(gating, 1)

                def gate_b(c):
                    dve.wait_ge(gating, c.at(GATE_STEPS, 4))
                    nc.vector.tensor_tensor(
                        above[:].rearrange("p t a i j -> p t (a i j)"), above[:].rearrange("p t a i j -> p t (a i j)"),
                        order[:].rearrange("p a i j -> p (a i j)").unsqueeze(1).broadcast_to([P, T, 2 * E * E]),
                        ALU.mult).then_inc(gating, 1)
                    dve.wait_ge(gating, c.at(GATE_STEPS, 5))
                    for t in range(T):
                        last = nc.vector.tensor_reduce(rank[:, t, :], above[:, t].rearrange("p a i j -> p i a j"),
                                                       AX.XY, ALU.add)
                    last.then_inc(gating, 1)
                    dve.wait_ge(gating, c.at(GATE_STEPS, 6))
                    dve.wait_ge(elog_ready, c.at(1, 1))
                    nc.vector.scalar_tensor_tensor(esel[:], rank[:], 1.5, elog[:], ALU.is_lt, ALU.mult) \
                        .then_inc(gating, 1)
                    nc.vector.tensor_reduce(eall[:], elog[:], AX.X, ALU.add)
                    dve.wait_ge(gating, c.at(GATE_STEPS, 7))
                    nc.vector.tensor_reduce(esum[:], esel[:], AX.X, ALU.add).then_inc(gating, 1)
                    dve.wait_ge(gating, c.at(GATE_STEPS, 8))
                    nc.vector.scalar_tensor_tensor(gden[:], eall[:], RANK_EPS, esum[:], ALU.mult, ALU.add) \
                        .then_inc(gating, 1)
                    dve.wait_ge(gating, c.at(GATE_STEPS, 9))
                    nc.vector.reciprocal(ginv[:], gden[:]).then_inc(gating, 1)
                    dve.wait_ge(gating, c.at(GATE_STEPS, 10))
                    nc.vector.tensor_tensor(gate[:, :, 0:E], esel[:], ginv[:].unsqueeze(2).broadcast_to([P, T, E]),
                                            ALU.mult).then_inc(gating, 1)

                def gate_c(c):
                    dve.wait_ge(gating, c.at(GATE_STEPS, 11))
                    r = cps[:, 0:T * NR].rearrange("p (t n) -> p t n", n=NR)
                    nc.vector.tensor_tensor(
                        aw[:, :, 0:AR].rearrange("p t (e r) -> p t e r", r=R),
                        r[:, :, 0:AR].rearrange("p t (e r) -> p t e r", r=R),
                        gate[:].unsqueeze(3).broadcast_to([P, T, E + 1, R]), ALU.mult).then_inc(gating, 1)

                def knorm_v(a):
                    dve.wait_ge(front_out, a.at(NFA, FRONT_ACT.index("v3") + 1))
                    nc.vector.tensor_tensor(zb[:], vraw[:, :, D:D + H], bbeta[:].unsqueeze(1).broadcast_to([P, T, H]),
                                            ALU.add).then_inc(knorm, 1)
                    dve.wait_ge(front_out, a.at(NFA, NFA))
                    nc.vector.tensor_reduce(kn2[:], ksq[:].rearrange("p t (h d) -> p t h d", d=DH), AX.X, ALU.add) \
                        .then_inc(kn2_done, 1)
                    dve.wait_ge(kn2_done, a.at(1, 1))
                    nc.vector.tensor_scalar(kn2c[:], kn2[:], EPS_NORM2, None, ALU.max).then_inc(knorm, 1)
                    dve.wait_ge(ez_ready, a.at(1, 1))
                    nc.vector.tensor_scalar(ez1[:], ez[:], 1.0, None, ALU.add).then_inc(beta_steps, 1)
                    dve.wait_ge(beta_steps, a.at(2, 1))
                    nc.vector.reciprocal(beta[:], ez1[:]).then_inc(beta_steps, 1)
                    dve.wait_ge(beta_steps, a.at(2, 2))
                    dve.wait_ge(rk_ready, a.at(1, 1))
                    nc.vector.scalar_tensor_tensor(vscale[:], beta[:], ROOT_SCALE, rk[:], ALU.mult, ALU.mult) \
                        .then_inc(knorm, 1)

                def run(a, b, c):
                    if b:
                        mask(b, 0, 0)
                    if a:
                        for t in range(T):
                            dve.wait_ge(h_ready, a.at(T, t + 1))
                            last = nc.vector.bn_stats(st1[:, t, :], h[a.parity][:, t, :])
                        last.then_inc(stats1, 1)
                        dve.wait_ge(stats1, a.at(1, 1))
                        stand(dve, vec_stood)
                        for t in range(T):
                            last = nc.vector.bn_aggr(mv1[:, t, :], st1[:, t, :])
                        last.then_inc(var1_ready, 1)
                    if b:
                        mask(b, 0, 1)
                    if a:
                        dve.wait_ge(var1_ready, a.at(1, 1))
                        dve.wait_ge(rstd1_ready, a.at(1, 1))
                        nc.vector.scalar_tensor_tensor(nmr1[:], mv1[:, :, 0], -1.0, rstd1[:], ALU.mult, ALU.mult) \
                            .then_inc(nmr1_ready, 1)
                    if b:
                        mask(b, 1, 0)
                        mask(b, 1, 1)
                        attn_out(b, 0)
                        state_out(b, 0)
                    if c:
                        gate_a(c)
                    if b:
                        mask(b, 2, 0)
                        mask(b, 2, 1)
                        residual1(b, 0)
                        attn_out(b, 1)
                        state_out(b, 1)
                    if a:
                        clamp_q(a, 0)
                    if c:
                        gate_b(c)
                    if b:
                        mask(b, 3, 0)
                    if a:
                        clamp_q(a, 1)
                    if b:
                        residual1(b, 1)
                        mask(b, 3, 1)
                    if c:
                        gate_c(c)
                    if b:
                        attn_out(b, 2)
                        state_out(b, 2)
                    if a:
                        knorm_v(a)
                    if b:
                        residual1(b, 2)
                    if c:
                        residual2(c, 0)
                    if b:
                        attn_out(b, 3)
                    if c:
                        residual2(c, 1)
                    if b:
                        residual1(b, 3)
                        dve.wait_ge(stats2, b.at(T, T))
                        stand(dve, vec_stood)
                        for t in range(T):
                            last = nc.vector.bn_aggr(mv2[:, t, :], st2[:, t, :])
                        last.then_inc(var2_ready, 1)
                    if c:
                        residual2(c, 2)
                        residual2(c, 3)
                    if b:
                        dve.wait_ge(var2_ready, b.at(1, 1))
                        dve.wait_ge(rstd2_ready, b.at(1, 1))
                        nc.vector.scalar_tensor_tensor(nmr2[:], mv2[:, :, 0], -1.0, rstd2[:], ALU.mult, ALU.mult) \
                            .then_inc(nmr2_ready, 1)

                steps(dve, run)




            @block.tensor
            def _(pe):
                pe.wait_ge(loaded, LOADED)

                def front_bank(a, name):
                    u = FRONT.index(name)
                    before = FRONT[u - 2]
                    lap = 0 if u >= 2 else -1
                    if before[0] == "n":
                        wait_for(pe, qn2_ready, a.at(KH, int(before[1]) + 1 + lap * KH))
                    else:
                        wait_for(pe, front_out, a.at(NFA, FRONT_ACT.index(before) + 1 + lap * NFA))
                    return front[u % 2]

                def a_x(a, k):
                    dst = front_bank(a, f"x{k}")
                    for t in range(T):
                        pe.wait_ge(xn_ready, a.at(T, t + 1))
                        mm = nc.tensor.transpose(dst[:, t * P:t * P + P], xn[:, t, k * P:k * P + P], ident[:])
                    mm.then_inc(front_ready, 1)

                def a_qk(a, name, w, m):
                    dst = front_bank(a, f"{name}{m}")
                    pe.wait_ge(front_out, a.at(NFA, KH))
                    for k in range(KH):
                        mm = nc.tensor.matmul(dst[:], w[:, k, m * P:m * P + P], xT[:, k, :],
                                              start=(k == 0), stop=(k == KH - 1))
                    mm.then_inc(front_ready, 1)

                def a_v(a, t):
                    dst = front_bank(a, f"v{t}")
                    for k in range(KH):
                        mm = nc.tensor.matmul(dst[:, 0:D + H], xT[:, k, t * P:t * P + P], wvb[:, k, :],
                                              start=(k == 0), stop=(k == KH - 1))
                    mm.then_inc(front_ready, 1)

                def a_norm(a, m):
                    dst = front_bank(a, f"n{m}")
                    pe.wait_ge(qsq_ready, a.at(KH, m + 1))
                    nc.tensor.matmul(dst[:], headmask[:], qsq[:, m, :], start=True, stop=True) \
                        .then_inc(front_ready, 1)

                def a_k(a, t):
                    dst = front_bank(a, f"t{t}")
                    pe.wait_ge(front_out, a.at(NFA, FRONT_ACT.index("k1") + 1))
                    for m in range(KH):
                        mm = nc.tensor.transpose(dst[:, m * P:m * P + P], kT[a.parity][:, m, t * P:t * P + P],
                                                 ident[:])
                    mm.then_inc(front_ready, 1)

                def b_scores(b, t, m):
                    if t == 0 and m == 0:
                        pe.wait_ge(qexp_landed[b.parity], b.at_half(16 * QEXP_DMAS, 16 * QEXP_DMAS))
                    for u in (2 * m, 2 * m + 1):
                        wait_for(pe, masked, b.at(T * UNITS, UNITS * t + u - 1))
                        slot = UH * (u % 2)
                        nc.tensor.matmul(score[u % 2][:], kT[b.parity][:, m, t * P:t * P + P],
                                         qexp[b.parity][:, m, slot:slot + UH, t * P:t * P + P],
                                         start=True, stop=True).then_inc(scored, 1)

                def b_heads(b, t):
                    if t == 0:
                        pe.wait_ge(vz_ready, b.at(T, T))
                    pe.wait_ge(masked, b.at(T * UNITS, UNITS * (t + 1)))
                    wait_for(pe, attn_ready, b.at(T, t - 1))
                    if t:
                        pe.wait_ge(state_ready, b.at(T - 1, t))
                    for m in range(KH):
                        if t:
                            nc.tensor.matmul(oT[:, t % 2, m, :], state[:, m, :], qT[b.parity][:, m, t * P:t * P + P],
                                             start=True, stop=False, skip_group_check=True)
                        for odd in range(2):
                            for g in range(4):
                                head = 2 * g + odd
                                mm = nc.tensor.matmul(
                                    oT[32 * g:32 * g + 32, t % 2, m, :],
                                    vz[b.parity][:, t, 4 * m + g, DH * odd:DH * odd + 2 * DH],
                                    probs[t % 2][:, 2 * m + head // UH, head % UH, :],
                                    start=(t == 0 and odd == 0), stop=(odd == 1), skip_group_check=True)
                    mm.then_inc(oT_ready, 1)

                def b_state(b, t):
                    wait_for(pe, state_ready, b.at(T - 1, t))
                    for m in range(KH):
                        mm = nc.tensor.matmul(kv[:, m, :], ktok[b.parity][:, t, m * P:m * P + P],
                                              v_heads(vz[b.parity], t, 4 * m, 4),
                                              start=(t == 0 and m == 0), stop=(t == T - 2),
                                              skip_group_check=True)
                    mm.then_inc(kv_ready, 1)

                def b_project(b, t):
                    pe.wait_ge(attn_ready, b.at(T, t + 1))
                    wait_for(pe, h2_ready, b.at(T, t))
                    for m in range(KH):
                        mm = nc.tensor.matmul(tok[:, 0, :], attnT[t % 2][:, m, :], wo[:, m, :],
                                              start=(m == 0), stop=(m == KH - 1))
                    mm.then_inc(wo_ready, 1)

                def c_y(c, k):
                    wait_for(pe, cps_out, c.at(3, k))
                    for t in range(T):
                        pe.wait_ge(yn_ready, c.at(T, t + 1))
                        mm = nc.tensor.transpose(cps[:, t * P:t * P + P], yn[:, t, k * P:k * P + P], ident[:])
                    mm.then_inc(cps_ready, 1)

                def c_lowrank(c):
                    pe.wait_ge(cps_out, c.at(3, 2))
                    for t in range(T):
                        for k in range(KH):
                            mm = nc.tensor.matmul(cps[:, t * NR:t * NR + NR], yT[:, k, t * P:t * P + P], war[:, k, :],
                                                  start=(k == 0), stop=(k == KH - 1))
                    mm.then_inc(cps_ready, 1)

                def c_turn(c):
                    pe.wait_ge(gating, c.at(GATE_STEPS, GATE_STEPS))
                    for t in range(T):
                        mm = nc.tensor.transpose(cps[0:BR, t * P:t * P + P], aw[:, t, :], ident[:])
                    mm.then_inc(cps_ready, 1)

                def c_ffn(c, t):
                    if t == 0:
                        pe.wait_ge(cps_out, c.at(3, 3))
                    wait_for(pe, out_ready, c.at(T, t))
                    for k in range(KH):
                        nc.tensor.matmul(tok[:, 1, :], yT[:, k, t * P:t * P + P], wbase[:, k, :],
                                         start=(k == 0), stop=False)
                    nc.tensor.matmul(tok[:, 1, :], awT[:, t * P:t * P + P], wb[:], start=False, stop=True) \
                        .then_inc(ffn_ready, 1)

                def run(a, b, c):
                    if b:
                        b_scores(b, 0, 0)
                    if c:
                        c_y(c, 0)
                    if b:
                        b_scores(b, 0, 1)
                    if c:
                        c_y(c, 1)
                    if b:
                        b_scores(b, 1, 0)
                    if a:
                        a_x(a, 0)
                        a_x(a, 1)
                    if b:
                        b_scores(b, 1, 1)
                    if c:
                        c_lowrank(c)
                    if a:
                        a_qk(a, "q", wq, 0)
                    if b:
                        b_heads(b, 0)
                        b_state(b, 0)
                    if a:
                        a_qk(a, "q", wq, 1)
                        a_qk(a, "k", wk, 0)
                    if b:
                        b_scores(b, 2, 0)
                    if a:
                        a_qk(a, "k", wk, 1)
                        a_v(a, 0)
                    if b:
                        b_scores(b, 2, 1)
                        b_project(b, 0)
                    if a:
                        a_v(a, 1)
                        a_norm(a, 0)
                    if b:
                        b_heads(b, 1)
                        b_state(b, 1)
                    if a:
                        a_v(a, 2)
                        a_v(a, 3)
                    if b:
                        b_scores(b, 3, 0)
                    if a:
                        a_norm(a, 1)
                    if b:
                        b_project(b, 1)
                        b_scores(b, 3, 1)
                    if a:
                        a_k(a, 0)
                        a_k(a, 1)
                    if c:
                        c_turn(c)
                    if b:
                        b_heads(b, 2)
                        b_state(b, 2)
                    if c:
                        c_ffn(c, 0)
                    if a:
                        a_k(a, 2)
                        a_k(a, 3)
                    if b:
                        b_project(b, 2)
                    if c:
                        c_ffn(c, 1)
                    if b:
                        b_heads(b, 3)
                    if c:
                        c_ffn(c, 2)
                    if b:
                        b_project(b, 3)
                    if c:
                        c_ffn(c, 3)

                steps(pe, run)


def kernel(x, L0_tok_weight, L0_tok_bias, L0_attn_Wq, L0_attn_Wk, L0_attn_Wv, L0_attn_Wo, L0_attn_Wb,
           L0_attn_bb, L0_ffn_base_W, L0_ffn_base_b, L0_ffn_shared_A, L0_ffn_shared_B, L0_ffn_routed_A,
           L0_ffn_routed_B, L0_ffn_router_W, L0_ffn_router_b):
    import concourse.bacc as bacc
    from concourse.bass_utils import run_bass_kernel_spmd

    def row(v):
        return np.asarray(v).reshape(-1)

    base_b = np.asarray(L0_ffn_base_b)[None, :]
    i, j = np.arange(E)[:, None], np.arange(E)[None, :]
    head = np.arange(P) // DH
    arrays = {
        "tokens": np.asarray(x).reshape(SEQS * T, P).T,
        "table": np.asarray(L0_tok_weight).T,
        "tok_bias": row(L0_tok_bias),
        "w_q": np.asarray(L0_attn_Wq),
        "w_k": np.asarray(L0_attn_Wk),
        "w_vb": np.concatenate([np.asarray(L0_attn_Wv), np.asarray(L0_attn_Wb)], axis=1),
        "bb": row(L0_attn_bb),
        "w_o": np.asarray(L0_attn_Wo),
        "w_base": np.asarray(L0_ffn_base_W).T,
        "w_ar": np.concatenate([np.asarray(L0_ffn_routed_A).reshape(E * R, D), np.asarray(L0_ffn_shared_A),
                                np.asarray(L0_ffn_router_W)], axis=0).T,
        "w_b": np.concatenate([np.asarray(L0_ffn_routed_B).transpose(0, 2, 1).reshape(E * R, D),
                               np.asarray(L0_ffn_shared_B).T, base_b], axis=0),
        "router_b": row(L0_ffn_router_b),
        "ident": np.eye(P, dtype=np.float32),
        "causal": np.triu(np.ones((P, P), np.float32)),
        "headmask": (head[:, None] == head[None, :]).astype(np.float32),
        "order": np.stack([j > i, j < i]).astype(np.float32).reshape(-1),
    }
    arrays = {name + "_in": np.ascontiguousarray(a) for name, a in arrays.items()}

    nc = bacc.Bacc("TRN2", target_bir_lowering=False, num_devices=1)
    args = [nc.dram_tensor(name, a.shape, U32 if name == "tokens_in" else mybir.dt.from_np(a.dtype),
                           kind="ExternalInput").ap() for name, a in arrays.items()]
    result = nc.dram_tensor("result", (SEQS * L, D), F32, kind="ExternalOutput").ap()
    build(nc, *args, result)
    r = run_bass_kernel_spmd(nc, [arrays], core_ids=[0])
    return r.results[0]["result"].reshape(SEQS, L, D)
```

```python
import numpy as np

import concourse.bass as bass
from concourse import mybir

F32 = mybir.dt.float32
BF16 = mybir.dt.bfloat16
U32 = mybir.dt.uint32
ALU = mybir.AluOpType
ACT = mybir.ActivationFunctionType
AX = mybir.AxisListType

P = 128
SEQS = 16
L = 512
T = L // P
D = 256
KH = D // P
H = 16
DH = D // H
HM = H // KH
PAIRS = H // 2
UNITS = 4
UH = H // UNITS
E = 6
R = 16
AR = E * R + R
NR = AR + E
BR = AR + 1
VZ = 48
EPS_LN = 1e-5
EPS_NORM2 = 1e-12 ** 2
LN_SCALE = 65536.0
ROOT_SCALE = 256.0
RANK_EPS = 1e-6

FRONT = ["x0", "x1", "q0", "q1", "k0", "k1", "v0", "n0", "v1", "n1", "v2", "v3", "t0", "t1", "t2", "t3"]
FRONT_ACT = [u for u in FRONT if u[0] != "n"]
NF, NFA = len(FRONT), len(FRONT_ACT)
GATE_STEPS = 12
KNORM_STEPS = 3
Q_PARTS = [0, 0, 0, 1, 1, 2]
K_PARTS = [0, 1, 2, 0, 1, 0]
PARTS = 3
SR = DH * len(Q_PARTS)


class Seq:

    def __init__(self, j, offset):
        self.number = j * 2 + offset
        self.parity = offset % 2
        self.half = j + offset // 2

    def at(self, per_sequence, k):
        return self.number * per_sequence + k

    def at_half(self, per_sequence, k):
        return self.half * per_sequence + k


def wait_for(engine, semaphore, value):
    if isinstance(value, int) and value <= 0:
        return
    engine.wait_ge(semaphore, value)


def stand(engine, semaphore):
    engine.sem_inc(semaphore, 1)


def v_heads(buffer, t, pair, n):
    x = buffer[:, t, pair:pair + n, :].rearrange("p g (three d) -> p g three d", d=DH)
    return x[:, :, 0:3:2, :]


def steps(engine, run):
    def step(j, s, loop=False):
        stages = ((s + 2, Seq(j, s + 2)), (s + 1, Seq(j, s + 1)), (s, Seq(j, s)), (s - 1, Seq(j, s - 1)))
        run(*[seq if loop or 0 <= number < SEQS else None for number, seq in stages])

    for s in range(-2, 2):
        step(0, s)
    with engine.Fori(0, (SEQS - 4) // 2) as j:
        step(j, 2, True)
        step(j, 3, True)
    for s in range(SEQS - 2, SEQS + 1):
        step(0, s)


def build(nc, tokens, table, tok_bias, w_q, w_k, w_vb, bb, w_o, w_base, w_ar, w_b, router_b,
          ident_in, causal_in, headmask_in, order_in, scratch, out):
    from contextlib import ExitStack

    with ExitStack() as ctx:
        def sb(name, shape, dt=F32):
            return ctx.enter_context(nc.sbuf_tensor(name, shape, dt))

        def ps(name, shape):
            return ctx.enter_context(nc.psum_tensor(name, shape, F32))

        def sem(name):
            return ctx.enter_context(nc.semaphore(name))

        idx_all = sb("idx_all", [P, SEQS * T], U32)
        bias_tok = sb("bias_tok", [P, D])
        wq = sb("wq", [P, KH, D])
        wk = sb("wk", [P, KH, D])
        wvb = sb("wvb", [P, KH, D + H])
        bbeta = sb("bbeta", [P, H])
        wo = sb("wo", [P, KH, D])
        wbase = sb("wbase", [P, KH, D])
        war = sb("war", [P, KH, NR])
        wb = sb("wb", [BR, D])
        brouter = sb("brouter", [P, E])
        ident = sb("ident", [P, P])
        causal = sb("causal", [P, P])
        headmask = sb("headmask", [P, P])
        order = sb("order", [P, 2, E, E])
        eps_ln = sb("eps_ln", [P, 1])
        idx = sb("idx", [P, T], U32)
        rows = sb("rows", [P, T, D])
        h = [sb(f"h{i}", [P, T, D]) for i in range(2)]
        st1 = sb("st1", [P, T, 6])
        mv1 = sb("mv1", [P, T, 2])
        lnv1 = sb("lnv1", [P, T])
        rstd1 = sb("rstd1", [P, T])
        nmr1 = sb("nmr1", [P, T])
        xn = sb("xn", [P, T, D])
        xT = sb("xT", [P, KH, L])
        qT = [sb(f"qT{i}", [P, KH, L]) for i in range(2)]
        kT = sb("kT", [P, KH, L])
        qpart = sb("qpart", [P, PARTS, KH, L], BF16)
        kpart = sb("kpart", [P, PARTS, KH, L], BF16)
        rest = sb("rest", [P, KH, L])
        qs = [sb(f"qs{i}", [SR, HM, KH, L], BF16) for i in range(2)]
        ks = [sb(f"ks{i}", [SR, HM, KH, L], BF16) for i in range(2)]
        qsq = sb("qsq", [P, KH, L])
        rq = [sb(f"rq{i}", [P, KH, L]) for i in range(2)]
        vraw = sb("vraw", [P, T, D + H])
        ktok = [sb(f"ktok{i}", [P, T, D]) for i in range(2)]
        ksq = rest[:].rearrange("p k (t d) -> p (k t) d", d=D)
        kn2 = sb("kn2", [P, T, H])
        kn2c = sb("kn2c", [P, T, H])
        kln = sb("kln", [P, T, H])
        rk = sb("rk", [P, T, H])
        zb = sb("zb", [P, T, H])
        ez = sb("ez", [P, T, H])
        ez1 = sb("ez1", [P, T, H])
        beta = sb("beta", [P, T, H])
        vscale = sb("vscale", [P, T, H])
        vz = [sb(f"vz{i}", [P, T, PAIRS, VZ]) for i in range(2)]
        probs = [sb(f"probs{i}", [P, UNITS, UH, P]) for i in range(2)]
        state = sb("state", [P, KH, P])
        attnT = [sb(f"attnT{i}", [P, KH, P]) for i in range(2)]
        h2 = [sb(f"h2_{i}", [P, T, D]) for i in range(2)]
        st2 = sb("st2", [P, T, 6])
        mv2 = sb("mv2", [P, T, 2])
        lnv2 = sb("lnv2", [P, T])
        rstd2 = sb("rstd2", [P, T])
        nmr2 = sb("nmr2", [P, T])
        yn = sb("yn", [P, T, D])
        yT = sb("yT", [P, KH, L])
        logit = sb("logit", [P, T, E])
        lmax = sb("lmax", [P, T])
        lsub = sb("lsub", [P, T, E])
        elog = sb("elog", [P, T, E])
        above = sb("above", [P, T, 2, E, E])
        rank = sb("rank", [P, T, E])
        esel = sb("esel", [P, T, E])
        esum = sb("esum", [P, T])
        eall = sb("eall", [P, T])
        gden = sb("gden", [P, T])
        ginv = sb("ginv", [P, T])
        gate = sb("gate", [P, T, E + 1])
        aw = sb("aw", [P, T, BR])
        awT = sb("awT", [BR, L])

        front = [ps(f"front{i}", [P, L]) for i in range(2)]
        score = [ps(f"score{i}", [P, UH, P]) for i in range(2)]
        oT = ps("oT", [P, KH, P])
        kv = ps("kv", [P, KH, P])
        tok = ps("tok", [P, D])
        cps = ps("cps", [P, L])

        loaded = sem("loaded")
        idx_loaded = sem("idx_loaded")
        bias_loaded = sem("bias_loaded")
        gathered = sem("gathered")
        qpart_written = sem("qpart_written")
        kpart_written = sem("kpart_written")
        stack_landed = [sem(f"stack_landed{i}") for i in range(2)]
        stored = sem("stored")
        pool_set = sem("pool_set")
        idx_copied = sem("idx_copied")
        pool_stood = sem("pool_stood")
        rows_ready = sem("rows_ready")
        xn_ready = sem("xn_ready")
        yn_ready = sem("yn_ready")
        vz_ready = sem("vz_ready")
        qlow_ready = sem("qlow_ready")
        klow_ready = sem("klow_ready")
        front_ready = sem("front_ready")
        scored = sem("scored")
        oT_ready = sem("oT_ready")
        kv_ready = sem("kv_ready")
        wo_ready = sem("wo_ready")
        cps_ready = sem("cps_ready")
        ffn_ready = sem("ffn_ready")
        front_out = sem("front_out")
        h_ready = sem("h_ready")
        xn_ready_act = sem("xn_ready_act")
        qmid_ready = sem("qmid_ready")
        kmid_ready = sem("kmid_ready")
        qsq_ready = sem("qsq_ready")
        ln1_done = sem("ln1_done")
        rstd1_ready = sem("rstd1_ready")
        qln_done = sem("qln_done")
        rq_ready = sem("rq_ready")
        ez_ready = sem("ez_ready")
        kln_done = sem("kln_done")
        rk_ready = sem("rk_ready")
        ln2_done = sem("ln2_done")
        rstd2_ready = sem("rstd2_ready")
        cps_out = sem("cps_out")
        elog_ready = sem("elog_ready")
        vec_set = sem("vec_set")
        stats1 = sem("stats1")
        var1_ready = sem("var1_ready")
        nmr1_ready = sem("nmr1_ready")
        qn2_ready = sem("qn2_ready")
        qrest_ready = sem("qrest_ready")
        krest_ready = sem("krest_ready")
        knorm = sem("knorm")
        kn2_done = sem("kn2_done")
        beta_steps = sem("beta_steps")
        masked = sem("masked")
        attn_ready = sem("attn_ready")
        state_ready = sem("state_ready")
        h2_ready = sem("h2_ready")
        stats2 = sem("stats2")
        var2_ready = sem("var2_ready")
        nmr2_ready = sem("nmr2_ready")
        gating = sem("gating")
        out_ready = sem("out_ready")
        vec_stood = sem("vec_stood")

        out_t = out.rearrange("(s t p) d -> s p t d", s=SEQS, t=T)

        loads = [(ident[:], ident_in),
                 (wq[:], w_q.rearrange("(k p) m -> p k m", p=P)), (wk[:], w_k.rearrange("(k p) m -> p k m", p=P)),
                 (wvb[:], w_vb.rearrange("(k p) m -> p k m", p=P)), (causal[:], causal_in),
                 (headmask[:], headmask_in), (bbeta[:], bb.partition_broadcast(P)),
                 (wo[:], w_o.rearrange("(k p) m -> p k m", p=P)),
                 (wbase[:], w_base.rearrange("(k p) m -> p k m", p=P)),
                 (war[:], w_ar.rearrange("(k p) m -> p k m", p=P)), (wb[:], w_b),
                 (brouter[:], router_b.partition_broadcast(P)),
                 (order[:].rearrange("p a i j -> p (a i j)"), order_in.partition_broadcast(P))]
        LOADED = 16 * len(loads)

        with nc.Block() as block:
            @block.sync
            def _(sp):
                sp.dma_start(idx_all[:], tokens).then_inc(idx_loaded, 16)
                sp.dma_start(bias_tok[:], tok_bias.partition_broadcast(P)).then_inc(bias_loaded, 16)
                for dst, src in loads:
                    sp.dma_start(dst, src).then_inc(loaded, 16)

                def stack(a, x, part, low_ready, written, stacked, parts):
                    sp.wait_ge(low_ready, a.at(1, 1))
                    for i in range(PARTS):
                        sp.dma_start(scratch[a.parity, x, i], part[:, i, :, :].rearrange("p k l -> p (k l)")) \
                          .then_inc(written, 16)
                    sp.wait_ge(written, a.at(16 * PARTS, 16 * PARTS))
                    wait_for(sp, scored, a.at(T * UNITS, -T * UNITS))
                    for block_, i in enumerate(parts):
                        sp.dma_start(stacked[DH * block_:DH * block_ + DH].rearrange("p h k l -> p (h k l)"),
                                     scratch[a.parity, x, i].rearrange("(d h) n -> d (h n)", d=DH)) \
                          .then_inc(stack_landed[a.parity], 16)

                def run(n, a, b, c):
                    if a:
                        stack(a, 0, qpart, qlow_ready, qpart_written, qs[a.parity], Q_PARTS)
                        stack(a, 1, kpart, klow_ready, kpart_written, ks[a.parity], K_PARTS)
                    if c:
                        sp.wait_ge(out_ready, c.at(T, T))
                        sp.dma_start(out_t[c.number], h2[c.parity][:]).then_inc(stored, 16)

                steps(sp, run)
                sp.wait_ge(stored, 16 * SEQS)

            @block.gpsimd
            def _(pool):
                def gather(n):
                    nc.gpsimd.tensor_copy(idx[:], idx_all[:, bass.ds(n * T, T)]).then_inc(idx_copied, 1)
                    pool.wait_ge(idx_copied, n + 1)
                    stand(pool, pool_stood)
                    for t in range(T):
                        nc.gpsimd.indirect_dma_start(
                            out=rows[:, t, :], out_offset=None, in_=table,
                            in_offset=bass.IndirectOffsetOnAxis(ap=idx[:, t:t + 1], axis=0),
                        ).then_inc(gathered, 16)

                pool.wait_ge(idx_loaded, 16)
                gather(0)
                nc.gpsimd.memset(vz[0][:], 0.0)
                nc.gpsimd.memset(vz[1][:], 0.0)
                nc.gpsimd.memset(gate[:], 1.0)
                nc.gpsimd.memset(aw[:], 1.0).then_inc(pool_set, 1)
                pool.wait_ge(pool_set, 1)

                def low(a, part, mid_ready, low_ready):
                    pool.wait_ge(mid_ready, a.at(1, 1))
                    nc.gpsimd.tensor_tensor(part[:, 2, :, :], rest[:], part[:, 1, :, :], ALU.subtract) \
                        .then_inc(low_ready, 1)

                def run(n, a, b, c):
                    if n:
                        wait_for(pool, h_ready, n.at(T, 0))
                        if not (isinstance(n.number, int) and n.number == 0):
                            gather(n.number)
                    if c:
                        pool.wait_ge(nmr2_ready, c.at(1, 1))
                        stand(pool, pool_stood)
                        for t in range(T):
                            nc.gpsimd.tensor_scalar(yn[:, t, :], h2[c.parity][:, t, :], rstd2[:, t:t + 1],
                                                    nmr2[:, t:t + 1], ALU.mult, ALU.add).then_inc(yn_ready, 1)
                    if n:
                        if isinstance(n.number, int) and n.number == 0:
                            pool.wait_ge(bias_loaded, 16)
                        pool.wait_ge(gathered, n.at(16 * T, 16 * T))
                        for t in range(T):
                            nc.gpsimd.tensor_tensor(rows[:, t, :], rows[:, t, :], bias_tok[:],
                                                    ALU.add).then_inc(rows_ready, 1)
                    if a:
                        low(a, qpart, qmid_ready, qlow_ready)
                    if a:
                        low(a, kpart, kmid_ready, klow_ready)
                    if n:
                        pool.wait_ge(nmr1_ready, n.at(1, 1))
                        wait_for(pool, front_ready, n.at(NF, FRONT.index("x1") + 1 - NF))
                        stand(pool, pool_stood)
                        for t in range(T // 2):
                            nc.gpsimd.tensor_scalar(xn[:, t, :], rows[:, t, :], rstd1[:, t:t + 1],
                                                    nmr1[:, t:t + 1], ALU.mult, ALU.add).then_inc(xn_ready, 1)
                    if a:
                        pool.wait_ge(knorm, a.at(KNORM_STEPS, KNORM_STEPS))
                        wait_for(pool, oT_ready, a.at(T, -T))
                        for t in range(T):
                            v3 = vraw[:, t, 0:D].rearrange("p (g two d) -> p g two d", two=2, d=DH)
                            s3 = vscale[:, t, :].rearrange("p (g two) -> p g two", two=2).unsqueeze(3) \
                                .broadcast_to([P, PAIRS, 2, DH])
                            nc.gpsimd.tensor_tensor(v_heads(vz[a.parity], t, 0, PAIRS), v3, s3, ALU.mult) \
                                .then_inc(vz_ready, 1)

                steps(pool, run)

            @block.scalar
            def _(act):
                nc.scalar.preload_act_table_set("natural_log_exp_and_others")
                act.wait_ge(vec_set, 1)

                def out_of(a, name, dst, src):
                    nc.scalar.activation(dst, src, ACT.Copy).then_inc(front_out, 1)

                def ready(a, name):
                    act.wait_ge(front_ready, a.at(NF, FRONT.index(name) + 1))
                    return front[FRONT.index(name) % 2]

                def norm_q(a, m):
                    act.wait_ge(qn2_ready, a.at(KH, m + 1))
                    nc.scalar.activation(qsq[:, m, :], qsq[:, m, :], ACT.Ln, scale=LN_SCALE).then_inc(qln_done, 1)
                    act.wait_ge(qln_done, a.at(KH, m + 1))
                    nc.scalar.activation(rq[a.parity][:, m, :], qsq[:, m, :], ACT.Exp, scale=-0.5) \
                        .then_inc(rq_ready, 1)

                def take_v(a, t):
                    src = ready(a, f"v{t}")
                    wait_for(act, vz_ready, a.at(T, t + 1 - T))
                    out_of(a, f"v{t}", vraw[:, t, :], src[:, 0:D + H])

                def take_k(a, t):
                    src = ready(a, f"t{t}")
                    act.wait_ge(klow_ready, a.at(1, 1))
                    nc.scalar.activation(ksq[:, t, :], src[:, 0:D], ACT.Square)
                    out_of(a, f"t{t}", ktok[a.parity][:, t, :], src[:, 0:D])

                def take_q(a, m):
                    src = ready(a, f"q{m}")
                    nc.scalar.activation(qsq[:, m, :], src[:], ACT.Square).then_inc(qsq_ready, 1)
                    wait_for(act, qpart_written, a.at(16 * PARTS, 0))
                    nc.scalar.activation(qpart[:, 0, m, :], src[:], ACT.Copy)
                    out_of(a, f"q{m}", qT[a.parity][:, m, :], src[:])

                def take_kT(a, m):
                    src = ready(a, f"k{m}")
                    wait_for(act, kpart_written, a.at(16 * PARTS, 0))
                    nc.scalar.activation(kpart[:, 0, m, :], src[:], ACT.Copy)
                    out_of(a, f"k{m}", kT[:, m, :], src[:])

                def middle(a, part, rest_ready, mid_ready):
                    act.wait_ge(rest_ready, a.at(1, 1))
                    nc.scalar.activation(part[:, 1, :, :], rest[:], ACT.Copy).then_inc(mid_ready, 1)

                def rstd_1(n):
                    act.wait_ge(var1_ready, n.at(1, 1))
                    nc.scalar.activation(lnv1[:], mv1[:, :, 1], ACT.Ln, bias=eps_ln[:, 0:1]).then_inc(ln1_done, 1)
                    act.wait_ge(ln1_done, n.at(1, 1))
                    wait_for(act, xn_ready, n.at(T // 2, 0))
                    nc.scalar.activation(rstd1[:], lnv1[:], ACT.Exp, scale=-0.5).then_inc(rstd1_ready, 1)

                def norm_1(n):
                    act.wait_ge(nmr1_ready, n.at(1, 1))
                    wait_for(act, front_ready, n.at(NF, FRONT.index("x1") + 1 - NF))
                    for t in range(T // 2, T):
                        nc.scalar.activation(xn[:, t, :], rows[:, t, :], ACT.Identity,
                                             bias=nmr1[:, t:t + 1], scale=rstd1[:, t:t + 1]) \
                            .then_inc(xn_ready_act, 1)

                def run(n, a, b, c):
                    if a:
                        wait_for(act, xn_ready, a.at(T // 2, T // 2))
                        for t in range(T):
                            if t == 0:
                                wait_for(act, h2_ready, a.at(T, -T))
                            nc.scalar.activation(h[a.parity][:, t, :], rows[:, t, :], ACT.Copy).then_inc(h_ready, 1)
                        for k in range(KH):
                            out_of(a, f"x{k}", xT[:, k, :], ready(a, f"x{k}")[:])
                        take_q(a, 0)
                        take_q(a, 1)
                        take_kT(a, 0)
                        middle(a, qpart, qrest_ready, qmid_ready)
                        take_kT(a, 1)
                    if c:
                        act.wait_ge(cps_ready, c.at(4, 1))
                        nc.scalar.activation(yT[:, 0, :], cps[:], ACT.Copy).then_inc(cps_out, 1)
                        act.wait_ge(cps_ready, c.at(4, 2))
                        nc.scalar.activation(yT[:, 1, :], cps[:], ACT.Copy).then_inc(cps_out, 1)
                    if a:
                        middle(a, kpart, krest_ready, kmid_ready)
                    if n:
                        rstd_1(n)
                    if a:
                        take_v(a, 0)
                    if n:
                        norm_1(n)
                    if c:
                        act.wait_ge(gating, c.at(GATE_STEPS, 3))
                        nc.scalar.activation(elog[:], lsub[:], ACT.Exp).then_inc(elog_ready, 1)
                    if a:
                        norm_q(a, 0)
                        take_v(a, 1)
                        norm_q(a, 1)
                        take_v(a, 2)
                        take_v(a, 3)
                    if c:
                        act.wait_ge(cps_ready, c.at(4, 4))
                        nc.scalar.activation(awT[:], cps[0:BR, :], ACT.Copy).then_inc(cps_out, 1)
                    if a:
                        for t in range(T):
                            take_k(a, t)
                        act.wait_ge(knorm, a.at(KNORM_STEPS, 1))
                        nc.scalar.activation(ez[:], zb[:], ACT.Exp, scale=-1.0).then_inc(ez_ready, 1)
                        act.wait_ge(knorm, a.at(KNORM_STEPS, 2))
                        nc.scalar.activation(kln[:], kn2c[:], ACT.Ln, scale=LN_SCALE).then_inc(kln_done, 1)
                        act.wait_ge(kln_done, a.at(1, 1))
                        nc.scalar.activation(rk[:], kln[:], ACT.Exp, scale=-0.5).then_inc(rk_ready, 1)
                    if b:
                        act.wait_ge(var2_ready, b.at(1, 1))
                        nc.scalar.activation(lnv2[:], mv2[:, :, 1], ACT.Ln, bias=eps_ln[:, 0:1]).then_inc(ln2_done, 1)
                        act.wait_ge(ln2_done, b.at(1, 1))
                        nc.scalar.activation(rstd2[:], lnv2[:], ACT.Exp, scale=-0.5).then_inc(rstd2_ready, 1)

                steps(act, run)

            @block.vector
            def _(dve):
                nc.vector.memset(eps_ln[:], EPS_LN).then_inc(vec_set, 1)
                dve.wait_ge(vec_set, 1)
                dve.wait_ge(loaded, LOADED)
                dve.wait_ge(pool_set, 1)

                def mask(b, t, *units):
                    for u in units:
                        dve.wait_ge(scored, b.at(T * UNITS, UNITS * t + u + 1))
                        if u == 0:
                            wait_for(dve, oT_ready, b.at(T, t - 1))
                        nc.vector.tensor_tensor(
                            probs[t % 2][:, u, :, :], score[u % 2][:],
                            causal[:].unsqueeze(1).broadcast_to([P, UH, P]), ALU.mult).then_inc(masked, 1)

                def attn_out(b, t):
                    dve.wait_ge(oT_ready, b.at(T, t + 1))
                    wait_for(dve, wo_ready, b.at(T, t - 1))
                    if t == 0:
                        dve.wait_ge(rq_ready, b.at(KH, KH))
                    nc.vector.scalar_tensor_tensor(
                        attnT[t % 2][:], oT[:], ROOT_SCALE, rq[b.parity][:, :, t * P:t * P + P],
                        ALU.mult, ALU.mult).then_inc(attn_ready, 1)

                def state_out(b, t):
                    dve.wait_ge(kv_ready, b.at(T - 1, t + 1))
                    nc.vector.tensor_tensor(state[:], kv[:], headmask[:].unsqueeze(1).broadcast_to([P, KH, P]),
                                            ALU.mult).then_inc(state_ready, 1)

                def residual1(b, t):
                    dve.wait_ge(wo_ready, b.at(T, t + 1))
                    if t == 0:
                        wait_for(dve, stored, b.at(16, -16))
                    nc.vector.tensor_tensor(h2[b.parity][:, t, :], tok[:], h[b.parity][:, t, :],
                                            ALU.add).then_inc(h2_ready, 1)
                    dve.wait_ge(h2_ready, b.at(T, t + 1))
                    nc.vector.bn_stats(st2[:, t, :], h2[b.parity][:, t, :]).then_inc(stats2, 1)

                def residual2(c, t):
                    dve.wait_ge(ffn_ready, c.at(T, t + 1))
                    y = h2[c.parity][:, t, :]
                    nc.vector.tensor_tensor(y, (tok if t % 2 else cps)[:, 0:D], y,
                                            ALU.add).then_inc(out_ready, 1)

                def clamp_q(a, m):
                    name = f"n{m}"
                    dve.wait_ge(front_ready, a.at(NF, FRONT.index(name) + 1))
                    nc.vector.tensor_scalar(qsq[:, m, :], front[FRONT.index(name) % 2][:], EPS_NORM2, None,
                                            ALU.max).then_inc(qn2_ready, 1)

                def gate_a(c):
                    dve.wait_ge(cps_ready, c.at(4, 3))
                    r = cps[:, 0:T * NR].rearrange("p (t n) -> p t n", n=NR)
                    nc.vector.tensor_tensor(logit[:], r[:, :, AR:NR], brouter[:].unsqueeze(1).broadcast_to([P, T, E]),
                                            ALU.add).then_inc(gating, 1)
                    dve.wait_ge(gating, c.at(GATE_STEPS, 1))
                    nc.vector.tensor_reduce(lmax[:], logit[:], AX.X, ALU.max).then_inc(gating, 1)
                    dve.wait_ge(gating, c.at(GATE_STEPS, 2))
                    nc.vector.tensor_tensor(lsub[:], logit[:], lmax[:].unsqueeze(2).broadcast_to([P, T, E]),
                                            ALU.subtract).then_inc(gating, 1)
                    for n, op in enumerate((ALU.is_gt, ALU.is_ge)):
                        for t in range(T):
                            last = nc.vector.tensor_tensor(
                                above[:, t, n, :, :], logit[:, t, :].unsqueeze(1).broadcast_to([P, E, E]),
                                logit[:, t, :].unsqueeze(2).broadcast_to([P, E, E]), op)
                    last.then_inc(gating, 1)

                def gate_b(c):
                    dve.wait_ge(gating, c.at(GATE_STEPS, 4))
                    nc.vector.tensor_tensor(
                        above[:].rearrange("p t a i j -> p t (a i j)"), above[:].rearrange("p t a i j -> p t (a i j)"),
                        order[:].rearrange("p a i j -> p (a i j)").unsqueeze(1).broadcast_to([P, T, 2 * E * E]),
                        ALU.mult).then_inc(gating, 1)
                    dve.wait_ge(gating, c.at(GATE_STEPS, 5))
                    for t in range(T):
                        last = nc.vector.tensor_reduce(rank[:, t, :], above[:, t].rearrange("p a i j -> p i a j"),
                                                       AX.XY, ALU.add)
                    last.then_inc(gating, 1)
                    dve.wait_ge(gating, c.at(GATE_STEPS, 6))
                    dve.wait_ge(elog_ready, c.at(1, 1))
                    nc.vector.scalar_tensor_tensor(esel[:], rank[:], 1.5, elog[:], ALU.is_lt, ALU.mult) \
                        .then_inc(gating, 1)
                    nc.vector.tensor_reduce(eall[:], elog[:], AX.X, ALU.add)
                    dve.wait_ge(gating, c.at(GATE_STEPS, 7))
                    nc.vector.tensor_reduce(esum[:], esel[:], AX.X, ALU.add).then_inc(gating, 1)
                    dve.wait_ge(gating, c.at(GATE_STEPS, 8))
                    nc.vector.scalar_tensor_tensor(gden[:], eall[:], RANK_EPS, esum[:], ALU.mult, ALU.add) \
                        .then_inc(gating, 1)
                    dve.wait_ge(gating, c.at(GATE_STEPS, 9))
                    nc.vector.reciprocal(ginv[:], gden[:]).then_inc(gating, 1)
                    dve.wait_ge(gating, c.at(GATE_STEPS, 10))
                    nc.vector.tensor_tensor(gate[:, :, 0:E], esel[:], ginv[:].unsqueeze(2).broadcast_to([P, T, E]),
                                            ALU.mult).then_inc(gating, 1)

                def gate_c(c):
                    dve.wait_ge(gating, c.at(GATE_STEPS, 11))
                    r = cps[:, 0:T * NR].rearrange("p (t n) -> p t n", n=NR)
                    nc.vector.tensor_tensor(
                        aw[:, :, 0:AR].rearrange("p t (e r) -> p t e r", r=R),
                        r[:, :, 0:AR].rearrange("p t (e r) -> p t e r", r=R),
                        gate[:].unsqueeze(3).broadcast_to([P, T, E + 1, R]), ALU.mult).then_inc(gating, 1)

                def knorm_v(a):
                    dve.wait_ge(front_out, a.at(NFA, NFA))
                    nc.vector.tensor_reduce(kn2[:].rearrange("p t (k h) -> p (t k) h", k=KH),
                                            ksq.rearrange("p t (k d h) -> p (t k) h d", k=KH, d=DH), AX.X, ALU.add) \
                        .then_inc(kn2_done, 1)
                    dve.wait_ge(kn2_done, a.at(1, 1))
                    nc.vector.tensor_scalar(kn2c[:], kn2[:], EPS_NORM2, None, ALU.max).then_inc(knorm, 1)
                    dve.wait_ge(ez_ready, a.at(1, 1))
                    nc.vector.tensor_scalar(ez1[:], ez[:], 1.0, None, ALU.add).then_inc(beta_steps, 1)
                    dve.wait_ge(beta_steps, a.at(2, 1))
                    nc.vector.reciprocal(beta[:], ez1[:]).then_inc(beta_steps, 1)
                    dve.wait_ge(beta_steps, a.at(2, 2))
                    dve.wait_ge(rk_ready, a.at(1, 1))
                    nc.vector.scalar_tensor_tensor(vscale[:], beta[:], ROOT_SCALE, rk[:], ALU.mult, ALU.mult) \
                        .then_inc(knorm, 1)

                def remainder(a, src, part, slot_free, rest_ready, done):
                    dve.wait_ge(front_out, a.at(NFA, done))
                    wait_for(dve, slot_free[0], slot_free[1])
                    nc.vector.tensor_tensor(rest[:], src[:], part[:, 0, :, :], ALU.subtract).then_inc(rest_ready, 1)

                def shift(seq, mean_var, rstd, rstd_ready, nmr, nmr_ready):
                    dve.wait_ge(rstd_ready, seq.at(1, 1))
                    nc.vector.scalar_tensor_tensor(nmr[:], mean_var[:, :, 0], -1.0, rstd[:], ALU.mult, ALU.mult) \
                        .then_inc(nmr_ready, 1)

                def stats_1(n):
                    for t in range(T):
                        dve.wait_ge(rows_ready, n.at(T, t + 1))
                        last = nc.vector.bn_stats(st1[:, t, :], rows[:, t, :])
                    last.then_inc(stats1, 1)
                    dve.wait_ge(stats1, n.at(1, 1))
                    stand(dve, vec_stood)
                    for t in range(T):
                        last = nc.vector.bn_aggr(mv1[:, t, :], st1[:, t, :])
                    last.then_inc(var1_ready, 1)

                def beta_logits(a):
                    dve.wait_ge(front_out, a.at(NFA, FRONT_ACT.index("v3") + 1))
                    nc.vector.tensor_tensor(zb[:], vraw[:, :, D:D + H], bbeta[:].unsqueeze(1).broadcast_to([P, T, H]),
                                            ALU.add).then_inc(knorm, 1)

                def run(n, a, b, c):
                    if c:
                        shift(c, mv2, rstd2, rstd2_ready, nmr2, nmr2_ready)
                    if b:
                        mask(b, 0, 0, 1, 2, 3)
                    if a:
                        remainder(a, qT[a.parity], qpart, (klow_ready, a.at(1, 0)), qrest_ready,
                                  FRONT_ACT.index("q1") + 1)
                    if b:
                        mask(b, 1, 0)
                        attn_out(b, 0)
                        mask(b, 1, 1)
                        state_out(b, 0)
                        mask(b, 1, 2, 3)
                    if n:
                        stats_1(n)
                    if a:
                        remainder(a, kT, kpart, (qlow_ready, a.at(1, 1)), krest_ready, FRONT_ACT.index("k1") + 1)
                    if n:
                        shift(n, mv1, rstd1, rstd1_ready, nmr1, nmr1_ready)
                    if b:
                        mask(b, 2, 0)
                        attn_out(b, 1)
                        state_out(b, 1)
                        mask(b, 2, 1)
                        residual1(b, 0)
                        mask(b, 2, 2, 3)
                    if c:
                        gate_a(c)
                    if a:
                        clamp_q(a, 0)
                    if b:
                        mask(b, 3, 0)
                        attn_out(b, 2)
                        state_out(b, 2)
                        mask(b, 3, 1)
                        residual1(b, 1)
                        mask(b, 3, 2)
                    if a:
                        clamp_q(a, 1)
                    if b:
                        mask(b, 3, 3)
                    if c:
                        gate_b(c)
                    if a:
                        beta_logits(a)
                    if b:
                        attn_out(b, 3)
                    if c:
                        gate_c(c)
                    if b:
                        residual1(b, 2)
                        residual1(b, 3)
                        dve.wait_ge(stats2, b.at(T, T))
                        stand(dve, vec_stood)
                        for t in range(T):
                            last = nc.vector.bn_aggr(mv2[:, t, :], st2[:, t, :])
                        last.then_inc(var2_ready, 1)
                    if c:
                        residual2(c, 0)
                        residual2(c, 1)
                    if a:
                        knorm_v(a)
                    if c:
                        residual2(c, 2)
                        residual2(c, 3)

                steps(dve, run)




            @block.tensor
            def _(pe):
                pe.wait_ge(loaded, LOADED)

                def front_bank(a, name):
                    u = FRONT.index(name)
                    before = FRONT[u - 2]
                    lap = 0 if u >= 2 else -1
                    if before[0] == "n":
                        wait_for(pe, qn2_ready, a.at(KH, int(before[1]) + 1 + lap * KH))
                    else:
                        wait_for(pe, front_out, a.at(NFA, FRONT_ACT.index(before) + 1 + lap * NFA))
                    return front[u % 2]

                def a_x(a, k):
                    dst = front_bank(a, f"x{k}")
                    for t in range(T):
                        if t < T // 2:
                            pe.wait_ge(xn_ready, a.at(T // 2, t + 1))
                        else:
                            pe.wait_ge(xn_ready_act, a.at(T // 2, t + 1 - T // 2))
                        mm = nc.tensor.transpose(dst[:, t * P:t * P + P], xn[:, t, k * P:k * P + P], ident[:])
                    mm.then_inc(front_ready, 1)

                def a_qk(a, name, w, m):
                    dst = front_bank(a, f"{name}{m}")
                    pe.wait_ge(front_out, a.at(NFA, KH))
                    for k in range(KH):
                        mm = nc.tensor.matmul(dst[:], w[:, k, m * P:m * P + P], xT[:, k, :],
                                              start=(k == 0), stop=(k == KH - 1))
                    mm.then_inc(front_ready, 1)

                def a_v(a, t):
                    dst = front_bank(a, f"v{t}")
                    for k in range(KH):
                        mm = nc.tensor.matmul(dst[:, 0:D + H], xT[:, k, t * P:t * P + P], wvb[:, k, :],
                                              start=(k == 0), stop=(k == KH - 1))
                    mm.then_inc(front_ready, 1)

                def a_norm(a, m):
                    dst = front_bank(a, f"n{m}")
                    pe.wait_ge(qsq_ready, a.at(KH, m + 1))
                    nc.tensor.matmul(dst[:], headmask[:], qsq[:, m, :], start=True, stop=True) \
                        .then_inc(front_ready, 1)

                def a_k(a, t):
                    dst = front_bank(a, f"t{t}")
                    pe.wait_ge(front_out, a.at(NFA, FRONT_ACT.index("k1") + 1))
                    for m in range(KH):
                        mm = nc.tensor.transpose(dst[:, m * P:m * P + P], kT[:, m, t * P:t * P + P],
                                                 ident[:])
                    mm.then_inc(front_ready, 1)

                def b_scores(b, t, u):
                    if t == 0 and u == 0:
                        pe.wait_ge(stack_landed[b.parity], b.at_half(32 * len(Q_PARTS), 32 * len(Q_PARTS)))
                    wait_for(pe, masked, b.at(T * UNITS, UNITS * t + u - 1))
                    for i in range(UH):
                        m, head = divmod(u * UH + i, HM)
                        mm = nc.tensor.matmul(score[u % 2][:, i, :], ks[b.parity][:, head, m, t * P:t * P + P],
                                              qs[b.parity][:, head, m, t * P:t * P + P], start=True, stop=True)
                    mm.then_inc(scored, 1)

                def b_heads(b, t):
                    if t == 0:
                        pe.wait_ge(vz_ready, b.at(T, T))
                    pe.wait_ge(masked, b.at(T * UNITS, UNITS * (t + 1)))
                    wait_for(pe, attn_ready, b.at(T, t))
                    if t:
                        pe.wait_ge(state_ready, b.at(T - 1, t))
                    for m in range(KH):
                        if t:
                            nc.tensor.matmul(oT[:, m, :], state[:, m, :], qT[b.parity][:, m, t * P:t * P + P],
                                             start=True, stop=False, skip_group_check=True)
                        for odd in range(2):
                            for g in range(4):
                                head = 2 * g + odd
                                mm = nc.tensor.matmul(
                                    oT[32 * g:32 * g + 32, m, :],
                                    vz[b.parity][:, t, 4 * m + g, DH * odd:DH * odd + 2 * DH],
                                    probs[t % 2][:, 2 * m + head // UH, head % UH, :],
                                    start=(t == 0 and odd == 0), stop=(odd == 1), skip_group_check=True)
                    mm.then_inc(oT_ready, 1)

                def b_state(b, t):
                    wait_for(pe, state_ready, b.at(T - 1, t))
                    for m in range(KH):
                        mm = nc.tensor.matmul(kv[:, m, :], ktok[b.parity][:, t, m * P:m * P + P],
                                              v_heads(vz[b.parity], t, 4 * m, 4),
                                              start=(t == 0 and m == 0), stop=(t == T - 2),
                                              skip_group_check=True)
                    mm.then_inc(kv_ready, 1)

                def b_project(b, t):
                    pe.wait_ge(attn_ready, b.at(T, t + 1))
                    if t == 0:
                        wait_for(pe, out_ready, b.at(T, -T))
                    else:
                        pe.wait_ge(h2_ready, b.at(T, t))
                    for m in range(KH):
                        mm = nc.tensor.matmul(tok[:], attnT[t % 2][:, m, :], wo[:, m, :],
                                              start=(m == 0), stop=(m == KH - 1))
                    mm.then_inc(wo_ready, 1)

                def c_y(c, k):
                    if k == 0:
                        wait_for(pe, out_ready, c.at(T, 0))
                    else:
                        pe.wait_ge(cps_out, c.at(3, 1))
                    for t in range(T):
                        pe.wait_ge(yn_ready, c.at(T, t + 1))
                        mm = nc.tensor.transpose(cps[:, t * P:t * P + P], yn[:, t, k * P:k * P + P], ident[:])
                    mm.then_inc(cps_ready, 1)

                def c_lowrank(c, tiles):
                    pe.wait_ge(cps_out, c.at(3, 2))
                    for t in tiles:
                        for k in range(KH):
                            mm = nc.tensor.matmul(cps[:, t * NR:t * NR + NR], yT[:, k, t * P:t * P + P], war[:, k, :],
                                                  start=(k == 0), stop=(k == KH - 1))
                    if t == T - 1:
                        mm.then_inc(cps_ready, 1)

                def c_turn(c):
                    pe.wait_ge(gating, c.at(GATE_STEPS, GATE_STEPS))
                    for t in range(T):
                        mm = nc.tensor.transpose(cps[0:BR, t * P:t * P + P], aw[:, t, :], ident[:])
                    mm.then_inc(cps_ready, 1)

                def c_ffn(b, c, t):
                    if t == 0:
                        pe.wait_ge(cps_out, c.at(3, 3))
                    if t >= 2:
                        pe.wait_ge(out_ready, c.at(T, t - 1))
                    elif t == 1 and b:
                        pe.wait_ge(h2_ready, b.at(T, T))
                    dst = (tok if t % 2 else cps)[:, 0:D]
                    for k in range(KH):
                        nc.tensor.matmul(dst, yT[:, k, t * P:t * P + P], wbase[:, k, :], start=(k == 0), stop=False)
                    nc.tensor.matmul(dst, awT[:, t * P:t * P + P], wb[:], start=False, stop=True) \
                        .then_inc(ffn_ready, 1)

                def run(n, a, b, c):
                    if a:
                        a_x(a, 0)
                    if b:
                        b_scores(b, 0, 0)
                    if a:
                        a_x(a, 1)
                    if b:
                        b_scores(b, 0, 1)
                    if a:
                        a_qk(a, "q", wq, 0)
                    if b:
                        b_scores(b, 0, 2)
                    if a:
                        a_qk(a, "q", wq, 1)
                    if b:
                        b_scores(b, 0, 3)
                    if a:
                        a_qk(a, "k", wk, 0)
                    if b:
                        b_heads(b, 0)
                        b_scores(b, 1, 0)
                    if a:
                        a_qk(a, "k", wk, 1)
                    if b:
                        b_scores(b, 1, 1)
                    if c:
                        c_y(c, 0)
                    if b:
                        b_state(b, 0)
                        b_scores(b, 1, 2)
                    if c:
                        c_y(c, 1)
                    if b:
                        b_scores(b, 1, 3)
                    if a:
                        a_v(a, 0)
                    if b:
                        b_heads(b, 1)
                        b_state(b, 1)
                        b_scores(b, 2, 0)
                    if c:
                        c_lowrank(c, (0, 1))
                    if b:
                        b_scores(b, 2, 1)
                        b_project(b, 0)
                        b_scores(b, 2, 2)
                    if c:
                        c_lowrank(c, (2, 3))
                    if b:
                        b_scores(b, 2, 3)
                    if a:
                        a_norm(a, 0)
                    if b:
                        b_heads(b, 2)
                        b_state(b, 2)
                        b_scores(b, 3, 0)
                    if a:
                        a_v(a, 1)
                    if b:
                        b_scores(b, 3, 1)
                        b_project(b, 1)
                        b_scores(b, 3, 2)
                    if a:
                        a_norm(a, 1)
                    if b:
                        b_scores(b, 3, 3)
                    if a:
                        a_v(a, 2)
                        a_v(a, 3)
                    if b:
                        b_heads(b, 3)
                        b_project(b, 2)
                    if c:
                        c_turn(c)
                    if a:
                        a_k(a, 0)
                        a_k(a, 1)
                    if b:
                        b_project(b, 3)
                    if a:
                        a_k(a, 2)
                    if c:
                        c_ffn(b, c, 0)
                    if a:
                        a_k(a, 3)
                    if c:
                        c_ffn(b, c, 1)
                        c_ffn(b, c, 2)
                        c_ffn(b, c, 3)

                steps(pe, run)


def kernel(x, L0_tok_weight, L0_tok_bias, L0_attn_Wq, L0_attn_Wk, L0_attn_Wv, L0_attn_Wo, L0_attn_Wb,
           L0_attn_bb, L0_ffn_base_W, L0_ffn_base_b, L0_ffn_shared_A, L0_ffn_shared_B, L0_ffn_routed_A,
           L0_ffn_routed_B, L0_ffn_router_W, L0_ffn_router_b):
    import concourse.bacc as bacc
    from concourse.bass_utils import run_bass_kernel_spmd

    def row(v):
        return np.asarray(v).reshape(-1)

    def by_dimension(w):
        return np.asarray(w).reshape(D, KH, HM, DH).transpose(0, 1, 3, 2).reshape(D, D)

    base_b = np.asarray(L0_ffn_base_b)[None, :]
    i, j = np.arange(E)[:, None], np.arange(E)[None, :]
    head = np.arange(P) // DH
    arrays = {
        "tokens": np.asarray(x).reshape(SEQS * T, P).T,
        "table": np.asarray(L0_tok_weight).T,
        "tok_bias": row(L0_tok_bias),
        "w_q": by_dimension(L0_attn_Wq),
        "w_k": by_dimension(L0_attn_Wk),
        "w_vb": np.concatenate([np.asarray(L0_attn_Wv), np.asarray(L0_attn_Wb)], axis=1),
        "bb": row(L0_attn_bb),
        "w_o": np.asarray(L0_attn_Wo),
        "w_base": np.asarray(L0_ffn_base_W).T,
        "w_ar": np.concatenate([np.asarray(L0_ffn_routed_A).reshape(E * R, D), np.asarray(L0_ffn_shared_A),
                                np.asarray(L0_ffn_router_W)], axis=0).T,
        "w_b": np.concatenate([np.asarray(L0_ffn_routed_B).transpose(0, 2, 1).reshape(E * R, D),
                               np.asarray(L0_ffn_shared_B).T, base_b], axis=0),
        "router_b": row(L0_ffn_router_b),
        "ident": np.eye(P, dtype=np.float32),
        "causal": np.triu(np.ones((P, P), np.float32)),
        "headmask": (np.arange(P)[:, None] % HM == head[None, :]).astype(np.float32),
        "order": np.stack([j > i, j < i]).astype(np.float32).reshape(-1),
    }
    arrays = {name + "_in": np.ascontiguousarray(a) for name, a in arrays.items()}

    nc = bacc.Bacc("TRN2", target_bir_lowering=False, num_devices=1)
    args = [nc.dram_tensor(name, a.shape, U32 if name == "tokens_in" else mybir.dt.from_np(a.dtype),
                           kind="ExternalInput").ap() for name, a in arrays.items()]
    result = nc.dram_tensor("result", (SEQS * L, D), F32, kind="ExternalOutput").ap()
    scratch = nc.dram_tensor("scratch", (2, 2, PARTS, P, KH * L), BF16, kind="Internal").ap()
    build(nc, *args, scratch, result)
    r = run_bass_kernel_spmd(nc, [arrays], core_ids=[0])
    return r.results[0]["result"].reshape(SEQS, L, D)
```

```python
import numpy as np

import concourse.bass as bass
from concourse import mybir

F32 = mybir.dt.float32
BF16 = mybir.dt.bfloat16
F32R = mybir.dt.float32r
U32 = mybir.dt.uint32
ALU = mybir.AluOpType
ACT = mybir.ActivationFunctionType
AX = mybir.AxisListType

P = 128
SEQS = 16
L = 512
T = L // P
D = 256
KH = D // P
H = 16
DH = D // H
HM = H // KH
PAIRS = H // 2
UNITS = 4
UH = H // UNITS
E = 6
R = 16
AR = E * R + R
NR = AR + E
BR = AR + 1
VZ = 48
EPS_LN = 1e-5
EPS_NORM2 = 1e-12 ** 2
LN_SCALE = 65536.0
ROOT_SCALE = 256.0
RANK_EPS = 1e-6

FRONT = ["q0", "q1", "k0", "k1", "v0", "v1", "n0", "v2", "v3", "n1", "t0", "t1", "t2", "t3"]
FRONT_ACT = [u for u in FRONT if u[0] != "n"]
NF, NFA = len(FRONT), len(FRONT_ACT)
GATE_STEPS = 12
KNORM_STEPS = 3
Q_ORDER = {"high": 0, "middle": 1, "low": 2}
K_ORDER = {"high": 2, "middle": 1, "low": 0}
Q_BLOCKS = [(0, 3, 0), (3, 2, 0), (5, 1, 0)]
K_BLOCKS = [(0, 3, 0), (3, 2, 1), (5, 1, 2)]
BLOCKS = 6
PARTS = 3
STACK_INCS = 16 * (len(Q_BLOCKS) + len(K_BLOCKS))
SR = DH * BLOCKS


class Seq:

    def __init__(self, j, offset):
        self.number = j * 2 + offset
        self.parity = offset % 2
        self.half = j + offset // 2

    def at(self, per_sequence, k):
        return self.number * per_sequence + k

    def at_half(self, per_sequence, k):
        return self.half * per_sequence + k


def is_first(seq):
    return isinstance(seq.number, int) and seq.number == 0


def adds_bias_early(seq):
    return isinstance(seq.number, int) and seq.number < 2


def wait_for(engine, semaphore, value):
    if isinstance(value, int) and value <= 0:
        return
    engine.wait_ge(semaphore, value)


def stand(engine, semaphore):
    engine.sem_inc(semaphore, 1)


def v_heads(buffer, t, pair, n):
    x = buffer[:, t, pair:pair + n, :].rearrange("p g (three d) -> p g three d", d=DH)
    return x[:, :, 0:3:2, :]


def by_tile(transposed):
    return transposed[:].rearrange("p k (t l) -> p k t l", t=T)


def steps(engine, run):
    def step(j, s, loop=False):
        stages = ((s + 2, Seq(j, s + 2)), (s + 1, Seq(j, s + 1)), (s, Seq(j, s)), (s - 1, Seq(j, s - 1)))
        run(*[seq if loop or 0 <= number < SEQS else None for number, seq in stages])

    for s in range(-2, 2):
        step(0, s)
    with engine.Fori(0, (SEQS - 4) // 2) as j:
        step(j, 2, True)
        step(j, 3, True)
    for s in range(SEQS - 2, SEQS + 1):
        step(0, s)


def build(nc, tokens, table, tok_bias, w_q, w_k, w_vb, bb, w_o, w_base, w_ar, w_b, router_b,
          ident_in, causal_in, headmask_in, order_in, scratch, out):
    from contextlib import ExitStack

    with ExitStack() as ctx:
        def sb(name, shape, dt=F32):
            return ctx.enter_context(nc.sbuf_tensor(name, shape, dt))

        def ps(name, shape):
            return ctx.enter_context(nc.psum_tensor(name, shape, F32))

        def sem(name):
            return ctx.enter_context(nc.semaphore(name))

        idx_all = sb("idx_all", [P, SEQS * T], U32)
        bias_tok = sb("bias_tok", [P, D])
        wq = [sb(f"wq_{part}", [P, KH, D], F32R) for part in ("high", "low")]
        wk = [sb(f"wk_{part}", [P, KH, D], F32R) for part in ("high", "low")]
        wvb = [sb(f"wvb_{part}", [P, KH, D + H], F32R) for part in ("high", "low")]
        bbeta = sb("bbeta", [P, H])
        wo = sb("wo", [P, KH, D])
        wbase = sb("wbase", [P, KH, D])
        war = sb("war", [P, KH, NR])
        wb = sb("wb", [BR, D])
        brouter = sb("brouter", [P, E])
        ident = sb("ident", [P, P])
        causal = sb("causal", [P, P])
        headmask = sb("headmask", [P, P])
        headmask_r = sb("headmask_r", [P, P], F32R)
        order = sb("order", [P, E, 2, E])
        eps_ln = sb("eps_ln", [P, 1])
        idx = sb("idx", [P, T], U32)
        rows = sb("rows", [P, T, D])
        h = [sb(f"h{i}", [P, T, D]) for i in range(2)]
        st1 = sb("st1", [P, T, 6])
        mv1 = sb("mv1", [P, T, 2])
        lnv1 = sb("lnv1", [P, T])
        rstd1 = sb("rstd1", [P, T])
        nmr1 = sb("nmr1", [P, T])
        xn = sb("xn", [P, T, D])
        xT = xn[:].rearrange("p t (k l) -> p k t l", k=KH)
        xT_high = sb("xT_high", [P, KH, L], F32R)
        xT_low = sb("xT_low", [P, KH, L], F32R)
        qT = [sb(f"qT{i}", [P, KH, L]) for i in range(2)]
        kT = sb("kT", [P, KH, L])
        qpart = sb("qpart", [P, PARTS, KH, L], BF16)
        kpart = sb("kpart", [P, PARTS, KH, L], BF16)
        rest = sb("rest", [P, KH, L])
        qs = [sb(f"qs{i}", [SR, HM, KH, L], BF16) for i in range(2)]
        ks = [sb(f"ks{i}", [SR, HM, KH, L], BF16) for i in range(2)]
        rq = [sb(f"rq{i}", [P, KH, L]) for i in range(2)]
        qsq_part = [sb(f"qsq_{part}", [P, L], F32R) for part in ("high", "low")]
        w_raw = rest[:].rearrange("p k l -> p (k l)").rearrange("p (x k m) -> p x k m", x=2, k=KH)
        vraw = sb("vraw", [P, T, D + H])
        wvb_raw = vraw[:, 0:KH, :]
        ktok = sb("ktok", [P, T, D])
        ksq = rest[:].rearrange("p k (t d) -> p (k t) d", d=D)
        kn2 = sb("kn2", [P, T, H])
        kn2c = sb("kn2c", [P, T, H])
        kln = sb("kln", [P, T, H])
        rk = sb("rk", [P, T, H])
        zb = sb("zb", [P, T, H])
        ez = sb("ez", [P, T, H])
        ez1 = sb("ez1", [P, T, H])
        beta = sb("beta", [P, T, H])
        vscale = sb("vscale", [P, T, H])
        vz = [sb(f"vz{i}", [P, T, PAIRS, VZ]) for i in range(2)]
        probs = sb("probs", [P, UNITS, UH, P])
        state = sb("state", [P, KH, P])
        attnT = [sb(f"attnT{i}", [P, KH, P]) for i in range(2)]
        h2 = [sb(f"h2_{i}", [P, T, D]) for i in range(2)]
        st2 = sb("st2", [P, T, 6])
        mv2 = sb("mv2", [P, T, 2])
        lnv2 = sb("lnv2", [P, T])
        rstd2 = sb("rstd2", [P, T])
        nmr2 = sb("nmr2", [P, T])
        yn = sb("yn", [P, T, D])
        yT = sb("yT", [P, KH, L])
        logit = sb("logit", [P, T, E])
        lmax = sb("lmax", [P, T])
        lsub = sb("lsub", [P, T, E])
        elog = sb("elog", [P, T, E])
        above = sb("above", [P, T, E, 2, E])
        rank = sb("rank", [P, T, E])
        esel = sb("esel", [P, T, E])
        esum = sb("esum", [P, T])
        eall = sb("eall", [P, T])
        gden = sb("gden", [P, T])
        ginv = sb("ginv", [P, T])
        gate = sb("gate", [P, T, E + 1])
        aw = sb("aw", [P, T, BR])
        awT = sb("awT", [BR, L])

        front = [ps(f"front{i}", [P, L]) for i in range(2)]
        score = [ps(f"score{i}", [P, UH, P]) for i in range(2)]
        oT = ps("oT", [P, KH, P])
        kv = ps("kv", [P, KH, P])
        tok = ps("tok", [P, D])
        cps = ps("cps", [P, L])

        loaded = sem("loaded")
        idx_loaded = sem("idx_loaded")
        bias_loaded = sem("bias_loaded")
        ident_loaded = sem("ident_loaded")
        qk_loaded = sem("qk_loaded")
        gathered = sem("gathered")
        qpart_written = sem("qpart_written")
        kpart_written = sem("kpart_written")
        stack_landed = [sem(f"stack_landed{i}") for i in range(2)]
        stored = sem("stored")
        sp_stood = sem("sp_stood")
        pool_set = sem("pool_set")
        idx_copied = sem("idx_copied")
        pool_stood = sem("pool_stood")
        rows_ready = sem("rows_ready")
        xn_ready = sem("xn_ready")
        yn_ready = sem("yn_ready")
        pad_set = sem("pad_set")
        vz_ready = sem("vz_ready")
        qlow_ready = sem("qlow_ready")
        klow_ready = sem("klow_ready")
        qsq_low_ready = sem("qsq_low_ready")
        x_low_ready = sem("x_low_ready")
        x_turned = sem("x_turned")
        front_ready = sem("front_ready")
        scored = sem("scored")
        oT_ready = sem("oT_ready")
        kv_ready = sem("kv_ready")
        wo_ready = sem("wo_ready")
        cps_ready = sem("cps_ready")
        ffn_ready = sem("ffn_ready")
        front_out = sem("front_out")
        x_out = sem("x_out")
        h_ready = sem("h_ready")
        xn_ready_act = sem("xn_ready_act")
        qmid_ready = sem("qmid_ready")
        kmid_ready = sem("kmid_ready")
        qsq_high_ready = sem("qsq_high_ready")
        ln1_done = sem("ln1_done")
        rstd1_ready = sem("rstd1_ready")
        qln_done = sem("qln_done")
        rq_ready = sem("rq_ready")
        ez_ready = sem("ez_ready")
        kln_done = sem("kln_done")
        rk_ready = sem("rk_ready")
        ln2_done = sem("ln2_done")
        rstd2_ready = sem("rstd2_ready")
        yn_ready_act = sem("yn_ready_act")
        cps_out = sem("cps_out")
        elog_ready = sem("elog_ready")
        vec_set = sem("vec_set")
        w_high_ready = sem("w_high_ready")
        w_split = sem("w_split")
        wvb_high_ready = sem("wvb_high_ready")
        wvb_split = sem("wvb_split")
        headmask_ready = sem("headmask_ready")
        stats1 = sem("stats1")
        var1_ready = sem("var1_ready")
        nmr1_ready = sem("nmr1_ready")
        qn2_ready = sem("qn2_ready")
        qrest_ready = sem("qrest_ready")
        krest_ready = sem("krest_ready")
        knorm = sem("knorm")
        kn2_done = sem("kn2_done")
        beta_steps = sem("beta_steps")
        masked = sem("masked")
        attn_ready = sem("attn_ready")
        state_ready = sem("state_ready")
        h2_ready = sem("h2_ready")
        stats2 = sem("stats2")
        var2_ready = sem("var2_ready")
        nmr2_ready = sem("nmr2_ready")
        gating = sem("gating")
        out_ready = sem("out_ready")
        vec_stood = sem("vec_stood")

        def ffn_bank(a, b, t):
            if a:
                return (tok if t % 2 else cps)[:, 0:D]
            if b:
                return front[t // 2][:, t % 2 * D:(t % 2 + 1) * D]
            return front[t][:, 0:D] if t < 2 else (kv, oT)[t - 2][:].rearrange("p k l -> p (k l)")

        def y_bank(b, k):
            return cps if b or k == 0 else score[0][:].rearrange("p u l -> p (u l)")

        out_t = out.rearrange("(s t p) d -> s p t d", s=SEQS, t=T)

        loads = [(wvb_raw, w_vb.rearrange("(k p) m -> p k m", p=P)), (causal[:], causal_in),
                 (headmask[:], headmask_in), (bbeta[:], bb.partition_broadcast(P)),
                 (wo[:], w_o.rearrange("(k p) m -> p k m", p=P)),
                 (wbase[:], w_base.rearrange("(k p) m -> p k m", p=P)),
                 (war[:], w_ar.rearrange("(k p) m -> p k m", p=P)), (wb[:], w_b),
                 (brouter[:], router_b.partition_broadcast(P)),
                 (order[:].rearrange("p i a j -> p (i a j)"), order_in.partition_broadcast(P))]
        LOADED = 16 * len(loads)

        with nc.Block() as block:
            @block.sync
            def _(sp):
                sp.dma_start(idx_all[:], tokens).then_inc(idx_loaded, 16)
                sp.dma_start(bias_tok[:], tok_bias.partition_broadcast(P)).then_inc(bias_loaded, 16)
                sp.dma_start(ident[:], ident_in).then_inc(ident_loaded, 16)
                for i, w in enumerate((w_q, w_k)):
                    sp.dma_start(w_raw[:, i], w.rearrange("(k p) m -> p k m", p=P)).then_inc(qk_loaded, 16)
                for dst, src in loads:
                    sp.dma_start(dst, src).then_inc(loaded, 16)

                def stack(a, x, part, low_ready, written, stacked, blocks):
                    parts = scratch[a.parity, x]
                    sp.wait_ge(low_ready, a.at(1, 1))
                    sp.dma_start(parts.rearrange("i p n -> p i n"),
                                 part[:].rearrange("p i k l -> p i (k l)")).then_inc(written, 16)
                    sp.wait_ge(written, a.at(16, 16))
                    stand(sp, sp_stood)
                    wait_for(sp, scored, a.at(T * UNITS, -T * UNITS))
                    for block_, n, i in blocks:
                        sp.dma_start(stacked[DH * block_:DH * (block_ + n)].rearrange("p h k l -> p (h k l)"),
                                     parts[i:i + n].rearrange("i (d h) n -> (i d) (h n)", d=DH)) \
                          .then_inc(stack_landed[a.parity], 16)

                def run(n, a, b, c):
                    if a:
                        stack(a, 0, qpart, qlow_ready, qpart_written, qs[a.parity], Q_BLOCKS)
                        stack(a, 1, kpart, klow_ready, kpart_written, ks[a.parity], K_BLOCKS)
                    if c:
                        if b:
                            sp.wait_ge(out_ready, c.at(T, T))
                            sp.dma_start(out_t[c.number], h2[c.parity][:]).then_inc(stored, 16)
                        else:
                            for t in range(T):
                                sp.wait_ge(out_ready, c.at(T, t + 1))
                                sp.dma_start(out_t[c.number][:, t, :], h2[c.parity][:, t, :]).then_inc(stored, 16)

                steps(sp, run)
                sp.wait_ge(stored, 16 * (SEQS - 1 + T))

            @block.gpsimd
            def _(pool):
                def gather(n):
                    nc.gpsimd.tensor_copy(idx[:], idx_all[:, bass.ds(n * T, T)]).then_inc(idx_copied, 1)
                    pool.wait_ge(idx_copied, n + 1)
                    stand(pool, pool_stood)
                    for t in range(T):
                        nc.gpsimd.indirect_dma_start(
                            out=rows[:, t, :], out_offset=None, in_=table,
                            in_offset=bass.IndirectOffsetOnAxis(ap=idx[:, t:t + 1], axis=0),
                        ).then_inc(gathered, 16)

                pool.wait_ge(idx_loaded, 16)
                gather(0)
                nc.gpsimd.memset(gate[:], 1.0)
                nc.gpsimd.memset(aw[:], 1.0).then_inc(pool_set, 1)
                pool.wait_ge(pool_set, 1)
                nc.gpsimd.memset(vz[0][:], 0.0)
                nc.gpsimd.memset(vz[1][:], 0.0).then_inc(pad_set, 1)
                pool.wait_ge(pad_set, 1)

                def low(a, part, order_of, mid_ready, low_ready):
                    pool.wait_ge(mid_ready, a.at(1, 1))
                    nc.gpsimd.tensor_tensor(part[:, order_of["low"], :, :], rest[:],
                                            part[:, order_of["middle"], :, :], ALU.subtract) \
                        .then_inc(low_ready, 1)

                def qsq_low(a, m):
                    pool.wait_ge(qsq_high_ready, a.at(KH, m + 1))
                    nc.gpsimd.tensor_tensor(qsq_part[1][:], rq[a.parity][:, m, :], qsq_part[0][:], ALU.subtract) \
                        .then_inc(qsq_low_ready, 1)

                def norm_1(n):
                    pool.wait_ge(nmr1_ready, n.at(1, 1))
                    wait_for(pool, x_low_ready, n.at(1, 0))
                    stand(pool, pool_stood)
                    for t in range(T // 2):
                        nc.gpsimd.tensor_scalar(xn[:, t, :], rows[:, t, :], rstd1[:, t:t + 1],
                                                nmr1[:, t:t + 1], ALU.mult, ALU.add).then_inc(xn_ready, 1)

                def run(n, a, b, c):
                    if n:
                        wait_for(pool, h_ready, n.at(T, 0))
                        if not is_first(n):
                            gather(n.number)
                    if a:
                        low(a, qpart, Q_ORDER, qmid_ready, qlow_ready)
                    if n and not adds_bias_early(n):
                        pool.wait_ge(gathered, n.at(16 * T, 16 * T))
                        for t in range(T):
                            nc.gpsimd.tensor_tensor(rows[:, t, :], rows[:, t, :], bias_tok[:],
                                                    ALU.add).then_inc(rows_ready, 1)
                    if a:
                        qsq_low(a, 0)
                        if is_first(a):
                            norm_1(n)
                        low(a, kpart, K_ORDER, kmid_ready, klow_ready)
                        qsq_low(a, 1)
                    if n and not (a and is_first(a)):
                        norm_1(n)
                    if n:
                        if not is_first(n):
                            pool.wait_ge(x_out, n.at(KH, KH))
                            nc.gpsimd.tensor_tensor(by_tile(xT_low), xT, by_tile(xT_high), ALU.subtract) \
                                .then_inc(x_low_ready, 1)
                    if a:
                        pool.wait_ge(knorm, a.at(KNORM_STEPS, KNORM_STEPS))
                        wait_for(pool, oT_ready, a.at(T, -T))
                        for t in range(T):
                            v3 = vraw[:, t, 0:D].rearrange("p (g two d) -> p g two d", two=2, d=DH)
                            s3 = vscale[:, t, :].rearrange("p (g two) -> p g two", two=2).unsqueeze(3) \
                                .broadcast_to([P, PAIRS, 2, DH])
                            nc.gpsimd.tensor_tensor(v_heads(vz[a.parity], t, 0, PAIRS), v3, s3, ALU.mult) \
                                .then_inc(vz_ready, 1)

                    if b:
                        pool.wait_ge(nmr2_ready, b.at(1, 1))
                        wait_for(pool, cps_ready, b.at(4, -2))
                        stand(pool, pool_stood)
                        for t in range(T // 2):
                            nc.gpsimd.tensor_scalar(yn[:, t, :], h2[b.parity][:, t, :], rstd2[:, t:t + 1],
                                                    nmr2[:, t:t + 1], ALU.mult, ALU.add).then_inc(yn_ready, 1)
                steps(pool, run)

            @block.scalar
            def _(act):
                nc.scalar.preload_act_table_set("natural_log_exp_and_others")
                act.wait_ge(vec_set, 1)

                def out_of(a, name, dst, src):
                    nc.scalar.activation(dst, src, ACT.Copy).then_inc(front_out, 1)

                def ready(a, name):
                    act.wait_ge(front_ready, a.at(NF, FRONT.index(name) + 1))
                    return front[FRONT.index(name) % 2]

                def norm_q(a, m):
                    act.wait_ge(qn2_ready, a.at(KH, m + 1))
                    nc.scalar.activation(rq[a.parity][:, m, :], rq[a.parity][:, m, :], ACT.Ln, scale=LN_SCALE) \
                        .then_inc(qln_done, 1)
                    act.wait_ge(qln_done, a.at(KH, m + 1))
                    nc.scalar.activation(rq[a.parity][:, m, :], rq[a.parity][:, m, :], ACT.Exp, scale=-0.5) \
                        .then_inc(rq_ready, 1)

                def take_v(a, t):
                    src = ready(a, f"v{t}")
                    wait_for(act, vz_ready, a.at(T, t + 1 - T))
                    out_of(a, f"v{t}", vraw[:, t, :], src[:, 0:D + H])

                def take_k(a, t):
                    src = ready(a, f"t{t}")
                    act.wait_ge(klow_ready, a.at(1, 1))
                    nc.scalar.activation(ksq[:, t, :], src[:, 0:D], ACT.Square)
                    out_of(a, f"t{t}", ktok[:, t, :], src[:, 0:D])

                def take_q(a, m):
                    src = ready(a, f"q{m}")
                    wait_for(act, attn_ready, a.at(T, -T))
                    nc.scalar.activation(rq[a.parity][:, m, :], src[:], ACT.Square)
                    wait_for(act, qpart_written, a.at(16, 0))
                    nc.scalar.activation(qpart[:, Q_ORDER["high"], m, :], src[:], ACT.Copy)
                    out_of(a, f"q{m}", qT[a.parity][:, m, :], src[:])

                def take_kT(a, m):
                    src = ready(a, f"k{m}")
                    wait_for(act, kpart_written, a.at(16, 0))
                    nc.scalar.activation(kpart[:, K_ORDER["high"], m, :], src[:], ACT.Copy)
                    out_of(a, f"k{m}", kT[:, m, :], src[:])

                def qsq_high(a, m):
                    if m:
                        act.wait_ge(front_ready, a.at(NF, FRONT.index("n0") + 1))
                    else:
                        wait_for(act, front_ready, a.at(NF, FRONT.index("n1") + 1 - NF))
                    nc.scalar.activation(qsq_part[0][:], rq[a.parity][:, m, :], ACT.Copy).then_inc(qsq_high_ready, 1)

                def middle(a, part, rest_ready, mid_ready):
                    act.wait_ge(rest_ready, a.at(1, 1))
                    nc.scalar.activation(part, rest[:], ACT.Copy).then_inc(mid_ready, 1)

                def take_y(b, c, k):
                    act.wait_ge(cps_ready, c.at(4, k + 1))
                    nc.scalar.activation(yT[:, k, :], y_bank(b, k)[:, 0:L], ACT.Copy).then_inc(cps_out, 1)

                def turned_out(n, k):
                    act.wait_ge(x_turned, n.at(KH, k + 1))
                    nc.scalar.activation(xT_high[:, k, :], front[k][:], ACT.Copy)
                    nc.scalar.activation(xT[:, k], front[k][:].rearrange("p (t l) -> p t l", t=T), ACT.Copy).then_inc(x_out, 1)

                def rstd_1(n):
                    act.wait_ge(var1_ready, n.at(1, 1))
                    nc.scalar.activation(lnv1[:], mv1[:, :, 1], ACT.Ln, bias=eps_ln[:, 0:1]).then_inc(ln1_done, 1)
                    act.wait_ge(ln1_done, n.at(1, 1))
                    wait_for(act, xn_ready, n.at(T // 2, 0))
                    nc.scalar.activation(rstd1[:], lnv1[:], ACT.Exp, scale=-0.5).then_inc(rstd1_ready, 1)

                def norm_1(n):
                    act.wait_ge(nmr1_ready, n.at(1, 1))
                    wait_for(act, x_low_ready, n.at(1, 0))
                    for t in range(T // 2, T):
                        nc.scalar.activation(xn[:, t, :], rows[:, t, :], ACT.Identity,
                                             bias=nmr1[:, t:t + 1], scale=rstd1[:, t:t + 1]) \
                            .then_inc(xn_ready_act, 1)

                def run(n, a, b, c):
                    if a:
                        take_q(a, 0)
                        take_q(a, 1)
                        take_kT(a, 0)
                        middle(a, qpart[:, Q_ORDER["middle"]], qrest_ready, qmid_ready)
                    if c:
                        take_y(b, c, 0)
                    if a:
                        take_kT(a, 1)
                    if c:
                        take_y(b, c, 1)
                    if a:
                        take_v(a, 0)
                        qsq_high(a, 0)
                        if is_first(a):
                            rstd_1(n)
                            take_v(a, 1)
                            norm_1(n)
                        middle(a, kpart[:, K_ORDER["middle"]], krest_ready, kmid_ready)
                        if not is_first(a):
                            take_v(a, 1)
                    if c:
                        act.wait_ge(gating, c.at(GATE_STEPS, 3))
                        nc.scalar.activation(elog[:], lsub[:], ACT.Exp).then_inc(elog_ready, 1)
                    if a and is_first(a):
                        qsq_high(a, 1)
                        take_v(a, 2)
                    if n and not (a and is_first(a)):
                        rstd_1(n)
                    if a and not is_first(a):
                        qsq_high(a, 1)
                        take_v(a, 2)
                    if n and not (a and is_first(a)):
                        norm_1(n)
                    if a:
                        take_v(a, 3)
                        norm_q(a, 0)
                    if n:
                        turned_out(n, 0)
                    if a:
                        take_k(a, 0)
                    if n:
                        turned_out(n, 1)
                    if c:
                        act.wait_ge(cps_ready, c.at(4, 4))
                        nc.scalar.activation(awT[:], cps[0:BR, :], ACT.Copy).then_inc(cps_out, 1)
                    if a:
                        for t in range(1, T):
                            take_k(a, t)
                        act.wait_ge(knorm, a.at(KNORM_STEPS, 1))
                        nc.scalar.activation(ez[:], zb[:], ACT.Exp, scale=-1.0).then_inc(ez_ready, 1)
                    if b:
                        act.wait_ge(var2_ready, b.at(1, 1))
                        nc.scalar.activation(lnv2[:], mv2[:, :, 1], ACT.Ln, bias=eps_ln[:, 0:1]).then_inc(ln2_done, 1)
                        act.wait_ge(ln2_done, b.at(1, 1))
                        wait_for(act, yn_ready, b.at(T // 2, 0))
                        nc.scalar.activation(rstd2[:], lnv2[:], ACT.Exp, scale=-0.5).then_inc(rstd2_ready, 1)
                    if a:
                        norm_q(a, 1)
                        act.wait_ge(knorm, a.at(KNORM_STEPS, 2))
                        nc.scalar.activation(kln[:], kn2c[:], ACT.Ln, scale=LN_SCALE).then_inc(kln_done, 1)
                        act.wait_ge(kln_done, a.at(1, 1))
                        nc.scalar.activation(rk[:], kln[:], ACT.Exp, scale=-0.5).then_inc(rk_ready, 1)
                    if n:
                        for t in range(T):
                            wait_for(act, h2_ready, n.at(T, -2 * T + t + 1))
                            nc.scalar.activation(h[n.parity][:, t, :], rows[:, t, :], ACT.Copy).then_inc(h_ready, 1)
                    if b:
                        act.wait_ge(nmr2_ready, b.at(1, 1))
                        wait_for(act, cps_ready, b.at(4, -2))
                        for t in range(T // 2, T):
                            nc.scalar.activation(yn[:, t, :], h2[b.parity][:, t, :], ACT.Identity,
                                                 bias=nmr2[:, t:t + 1], scale=rstd2[:, t:t + 1]) \
                                .then_inc(yn_ready_act, 1)

                steps(act, run)

            @block.vector
            def _(dve):
                nc.vector.memset(eps_ln[:], EPS_LN).then_inc(vec_set, 1)
                dve.wait_ge(vec_set, 1)
                dve.wait_ge(qk_loaded, 16 * 2)
                for i, w in enumerate((wq, wk)):
                    nc.vector.tensor_copy(w[0][:], w_raw[:, i]).then_inc(w_high_ready, 1)
                    dve.wait_ge(w_high_ready, i + 1)
                    nc.vector.tensor_tensor(w[1][:], w_raw[:, i], w[0][:], ALU.subtract).then_inc(w_split, 1)

                def mask(b, t, *units):
                    for u in units:
                        dve.wait_ge(scored, b.at(T * UNITS, UNITS * t + u + 1))
                        if u == 0:
                            wait_for(dve, oT_ready, b.at(T, t))
                        nc.vector.tensor_tensor(
                            probs[:, u, :, :], score[u % 2][:],
                            causal[:].unsqueeze(1).broadcast_to([P, UH, P]), ALU.mult).then_inc(masked, 1)

                def attn_out(b, t):
                    dve.wait_ge(oT_ready, b.at(T, t + 1))
                    wait_for(dve, wo_ready, b.at(T, t - 1))
                    if t == 0:
                        dve.wait_ge(rq_ready, b.at(KH, KH))
                    nc.vector.scalar_tensor_tensor(
                        attnT[t % 2][:], oT[:], ROOT_SCALE, rq[b.parity][:, :, t * P:t * P + P],
                        ALU.mult, ALU.mult).then_inc(attn_ready, 1)

                def state_out(b, t):
                    dve.wait_ge(kv_ready, b.at(T - 1, t + 1))
                    nc.vector.tensor_tensor(state[:], kv[:], headmask[:].unsqueeze(1).broadcast_to([P, KH, P]),
                                            ALU.mult).then_inc(state_ready, 1)

                def residual1(b, t):
                    dve.wait_ge(wo_ready, b.at(T, t + 1))
                    if t == 0:
                        wait_for(dve, stored, b.at(16, -16))
                    nc.vector.tensor_tensor(h2[b.parity][:, t, :], tok[:], h[b.parity][:, t, :],
                                            ALU.add).then_inc(h2_ready, 1)
                    dve.wait_ge(h2_ready, b.at(T, t + 1))
                    nc.vector.bn_stats(st2[:, t, :], h2[b.parity][:, t, :]).then_inc(stats2, 1)

                def residual2(a, b, c, t):
                    if b and not a:
                        dve.wait_ge(ffn_ready, c.at(T, (t | 1) + 1))
                    else:
                        dve.wait_ge(ffn_ready, c.at(T, t + 1))
                    y = h2[c.parity][:, t, :]
                    nc.vector.tensor_tensor(y, ffn_bank(a, b, t), y, ALU.add).then_inc(out_ready, 1)

                def clamp_q(a, m):
                    name = f"n{m}"
                    dve.wait_ge(front_ready, a.at(NF, FRONT.index(name) + 1))
                    nc.vector.tensor_scalar(rq[a.parity][:, m, :], front[FRONT.index(name) % 2][:], EPS_NORM2, None,
                                            ALU.max).then_inc(qn2_ready, 1)

                def gate_a(c):
                    dve.wait_ge(cps_ready, c.at(4, 3))
                    r = cps[:, 0:T * NR].rearrange("p (t n) -> p t n", n=NR)
                    nc.vector.tensor_tensor(logit[:], r[:, :, AR:NR], brouter[:].unsqueeze(1).broadcast_to([P, T, E]),
                                            ALU.add).then_inc(gating, 1)
                    dve.wait_ge(gating, c.at(GATE_STEPS, 1))
                    nc.vector.tensor_reduce(lmax[:], logit[:], AX.X, ALU.max).then_inc(gating, 1)
                    dve.wait_ge(gating, c.at(GATE_STEPS, 2))
                    nc.vector.tensor_tensor(lsub[:], logit[:], lmax[:].unsqueeze(2).broadcast_to([P, T, E]),
                                            ALU.subtract).then_inc(gating, 1)
                    for n, op in enumerate((ALU.is_gt, ALU.is_ge)):
                        last = nc.vector.tensor_tensor(
                            above[:, :, :, n, :], logit[:].unsqueeze(2).broadcast_to([P, T, E, E]),
                            logit[:].unsqueeze(3).broadcast_to([P, T, E, E]), op)
                    last.then_inc(gating, 1)

                def gate_rank(c):
                    dve.wait_ge(gating, c.at(GATE_STEPS, 4))
                    flat = above[:].rearrange("p t i a j -> p t (i a j)")
                    nc.vector.tensor_tensor(
                        flat, flat,
                        order[:].rearrange("p i a j -> p (i a j)").unsqueeze(1).broadcast_to([P, T, 2 * E * E]),
                        ALU.mult).then_inc(gating, 1)
                    dve.wait_ge(gating, c.at(GATE_STEPS, 5))
                    nc.vector.tensor_reduce(rank[:].rearrange("p t i -> p (t i)"),
                                            above[:].rearrange("p t i a j -> p (t i) (a j)"), AX.X, ALU.add) \
                        .then_inc(gating, 1)

                def gate_b(c):
                    dve.wait_ge(gating, c.at(GATE_STEPS, 6))
                    dve.wait_ge(elog_ready, c.at(1, 1))
                    nc.vector.scalar_tensor_tensor(esel[:], rank[:], 1.5, elog[:], ALU.is_lt, ALU.mult) \
                        .then_inc(gating, 1)
                    nc.vector.tensor_reduce(eall[:], elog[:], AX.X, ALU.add)
                    dve.wait_ge(gating, c.at(GATE_STEPS, 7))
                    nc.vector.tensor_reduce(esum[:], esel[:], AX.X, ALU.add).then_inc(gating, 1)
                    dve.wait_ge(gating, c.at(GATE_STEPS, 8))
                    nc.vector.scalar_tensor_tensor(gden[:], eall[:], RANK_EPS, esum[:], ALU.mult, ALU.add) \
                        .then_inc(gating, 1)
                    dve.wait_ge(gating, c.at(GATE_STEPS, 9))
                    nc.vector.reciprocal(ginv[:], gden[:]).then_inc(gating, 1)
                    dve.wait_ge(gating, c.at(GATE_STEPS, 10))
                    nc.vector.tensor_tensor(gate[:, :, 0:E], esel[:], ginv[:].unsqueeze(2).broadcast_to([P, T, E]),
                                            ALU.mult).then_inc(gating, 1)

                def gate_c(c):
                    dve.wait_ge(gating, c.at(GATE_STEPS, 11))
                    r = cps[:, 0:T * NR].rearrange("p (t n) -> p t n", n=NR)
                    nc.vector.tensor_tensor(
                        aw[:, :, 0:AR].rearrange("p t (e r) -> p t e r", r=R),
                        r[:, :, 0:AR].rearrange("p t (e r) -> p t e r", r=R),
                        gate[:].unsqueeze(3).broadcast_to([P, T, E + 1, R]), ALU.mult).then_inc(gating, 1)

                def knorm_v(a):
                    dve.wait_ge(front_out, a.at(NFA, NFA))
                    nc.vector.tensor_reduce(kn2[:].rearrange("p t (k h) -> p (t k) h", k=KH),
                                            ksq.rearrange("p t (k d h) -> p (t k) h d", k=KH, d=DH), AX.X, ALU.add) \
                        .then_inc(kn2_done, 1)
                    dve.wait_ge(kn2_done, a.at(1, 1))
                    nc.vector.tensor_scalar(kn2c[:], kn2[:], EPS_NORM2, None, ALU.max).then_inc(knorm, 1)

                def beta_of(a):
                    dve.wait_ge(ez_ready, a.at(1, 1))
                    nc.vector.tensor_scalar(ez1[:], ez[:], 1.0, None, ALU.add).then_inc(beta_steps, 1)
                    dve.wait_ge(beta_steps, a.at(2, 1))
                    nc.vector.reciprocal(beta[:], ez1[:]).then_inc(beta_steps, 1)

                def v_factor(a):
                    dve.wait_ge(beta_steps, a.at(2, 2))
                    dve.wait_ge(rk_ready, a.at(1, 1))
                    nc.vector.scalar_tensor_tensor(vscale[:], beta[:], ROOT_SCALE, rk[:], ALU.mult, ALU.mult) \
                        .then_inc(knorm, 1)

                def remainder(a, src, part, high, slot_free, rest_ready, done):
                    dve.wait_ge(front_out, a.at(NFA, done))
                    wait_for(dve, slot_free[0], slot_free[1])
                    nc.vector.tensor_tensor(rest[:], src[:], part[:, high, :, :], ALU.subtract) \
                        .then_inc(rest_ready, 1)

                def shift(seq, mean_var, rstd, rstd_ready, nmr, nmr_ready):
                    dve.wait_ge(rstd_ready, seq.at(1, 1))
                    nc.vector.scalar_tensor_tensor(nmr[:], mean_var[:, :, 0], -1.0, rstd[:], ALU.mult, ALU.mult) \
                        .then_inc(nmr_ready, 1)

                def stats_1(n):
                    if adds_bias_early(n):
                        dve.wait_ge(bias_loaded, 16)
                        dve.wait_ge(gathered, n.at(16 * T, 16 * T))
                        for t in range(T):
                            nc.vector.tensor_tensor(rows[:, t, :], rows[:, t, :], bias_tok[:],
                                                    ALU.add).then_inc(rows_ready, 1)
                    for t in range(T):
                        dve.wait_ge(rows_ready, n.at(T, t + 1))
                        last = nc.vector.bn_stats(st1[:, t, :], rows[:, t, :])
                    last.then_inc(stats1, 1)
                    dve.wait_ge(stats1, n.at(1, 1))
                    stand(dve, vec_stood)
                    for t in range(T):
                        last = nc.vector.bn_aggr(mv1[:, t, :], st1[:, t, :])
                    last.then_inc(var1_ready, 1)

                def var_2(b):
                    dve.wait_ge(stats2, b.at(T, T))
                    stand(dve, vec_stood)
                    for t in range(T):
                        last = nc.vector.bn_aggr(mv2[:, t, :], st2[:, t, :])
                    last.then_inc(var2_ready, 1)

                def beta_logits(a):
                    dve.wait_ge(front_out, a.at(NFA, FRONT_ACT.index("v3") + 1))
                    nc.vector.tensor_tensor(zb[:], vraw[:, :, D:D + H], bbeta[:].unsqueeze(1).broadcast_to([P, T, H]),
                                            ALU.add).then_inc(knorm, 1)

                def run_draining(b, c):
                    mask(b, 1, 0)
                    attn_out(b, 0)
                    mask(b, 1, 1)
                    state_out(b, 0)
                    mask(b, 1, 2, 3)
                    mask(b, 2, 0)
                    attn_out(b, 1)
                    state_out(b, 1)
                    mask(b, 2, 1)
                    residual1(b, 0)
                    mask(b, 2, 2, 3)
                    gate_a(c)
                    mask(b, 3, 0)
                    attn_out(b, 2)
                    state_out(b, 2)
                    mask(b, 3, 1)
                    residual1(b, 1)
                    mask(b, 3, 2, 3)
                    gate_rank(c)
                    residual1(b, 2)
                    attn_out(b, 3)
                    gate_b(c)
                    gate_c(c)
                    residual1(b, 3)
                    var_2(b)
                    shift(b, mv2, rstd2, rstd2_ready, nmr2, nmr2_ready)
                    for t in range(T):
                        residual2(None, b, c, t)

                def run(n, a, b, c):
                    if b and not a:
                        return run_draining(b, c)
                    if a and is_first(a):
                        dve.wait_ge(x_out, KH)
                        nc.vector.tensor_tensor(by_tile(xT_low), xT, by_tile(xT_high), ALU.subtract) \
                            .then_inc(x_low_ready, 1)
                        dve.wait_ge(loaded, LOADED)
                        dve.wait_ge(pool_set, 1)
                        nc.vector.tensor_copy(headmask_r[:], headmask[:]).then_inc(headmask_ready, 1)
                        nc.vector.tensor_copy(wvb[0][:], wvb_raw).then_inc(wvb_high_ready, 1)
                        dve.wait_ge(wvb_high_ready, 1)
                        nc.vector.tensor_tensor(wvb[1][:], wvb_raw, wvb[0][:], ALU.subtract).then_inc(wvb_split, 1)
                    if a:
                        remainder(a, qT[a.parity], qpart, Q_ORDER["high"], (klow_ready, a.at(1, 0)), qrest_ready,
                                  FRONT_ACT.index("q1") + 1)
                    if b and is_first(b):
                        mask(b, 0, 0, 1, 2, 3)
                    if b:
                        mask(b, 1, 0)
                        attn_out(b, 0)
                        mask(b, 1, 1)
                        state_out(b, 0)
                        mask(b, 1, 2, 3)
                    if a and is_first(a):
                        stats_1(n)
                        shift(n, mv1, rstd1, rstd1_ready, nmr1, nmr1_ready)
                    if a:
                        remainder(a, kT, kpart, K_ORDER["high"], (qlow_ready, a.at(1, 1)), krest_ready,
                                  FRONT_ACT.index("k1") + 1)
                    if a and is_first(a):
                        clamp_q(a, 0)
                    elif n:
                        stats_1(n)
                    if b:
                        mask(b, 2, 0)
                        attn_out(b, 1)
                        state_out(b, 1)
                        mask(b, 2, 1, 2, 3)
                    if a and not is_first(a):
                        clamp_q(a, 0)
                    if b:
                        residual1(b, 0)
                    if c:
                        gate_a(c)
                    if c:
                        gate_rank(c)
                    if n and not (a and is_first(a)):
                        shift(n, mv1, rstd1, rstd1_ready, nmr1, nmr1_ready)
                    if b:
                        mask(b, 3, 0)
                        attn_out(b, 2)
                        state_out(b, 2)
                        mask(b, 3, 1, 2, 3)
                        residual1(b, 1)
                    if a:
                        clamp_q(a, 1)
                    if c:
                        gate_b(c)
                    if b:
                        attn_out(b, 3)
                    if c:
                        gate_c(c)
                    if b:
                        residual1(b, 2)
                    if a:
                        beta_logits(a)
                    if b:
                        residual1(b, 3)
                        var_2(b)
                    if a and b:
                        mask(a, 0, 0)
                    if c:
                        residual2(a, b, c, 0)
                    if a and b:
                        mask(a, 0, 1)
                    if a:
                        knorm_v(a)
                    if c:
                        residual2(a, b, c, 1)
                    if a:
                        beta_of(a)
                        v_factor(a)
                    if b:
                        shift(b, mv2, rstd2, rstd2_ready, nmr2, nmr2_ready)
                    if a and b:
                        mask(a, 0, 2)
                    if c:
                        residual2(a, b, c, 2)
                    if a and b:
                        mask(a, 0, 3)
                    if c:
                        residual2(a, b, c, 3)

                steps(dve, run)

            @block.tensor
            def _(pe):
                pe.wait_ge(ident_loaded, 16)

                def front_bank(a, name):
                    u = FRONT.index(name)
                    before = FRONT[u - 2]
                    lap = 0 if u >= 2 else -1
                    if before[0] == "n":
                        wait_for(pe, qn2_ready, a.at(KH, int(before[1]) + 1 + lap * KH))
                    else:
                        wait_for(pe, front_out, a.at(NFA, FRONT_ACT.index(before) + 1 + lap * NFA))
                    return front[u % 2]

                def n_x(n, a, k):
                    if a:
                        if k == 0:
                            pe.wait_ge(front_out, a.at(NFA, FRONT_ACT.index("v3") + 1))
                        else:
                            pe.wait_ge(qn2_ready, a.at(KH, KH))
                    for t in range(T):
                        if t < T // 2:
                            pe.wait_ge(xn_ready, n.at(T // 2, t + 1))
                        else:
                            pe.wait_ge(xn_ready_act, n.at(T // 2, t + 1 - T // 2))
                        mm = nc.tensor.transpose(front[k][:, t * P:t * P + P], xn[:, t, k * P:k * P + P], ident[:])
                    mm.then_inc(x_turned, 1)

                def a_qk(a, name, w, m):
                    dst = front_bank(a, f"{name}{m}")
                    if is_first(a):
                        pe.wait_ge(w_split, 2)
                    pe.wait_ge(x_out, a.at(KH, KH))
                    products = ((0, xT_high), (1, xT_high), (0, xT_low))
                    for i, (w_part, x) in enumerate(products):
                        if i == len(products) - 1:
                            pe.wait_ge(x_low_ready, a.at(1, 1))
                        for k in range(KH):
                            mm = nc.tensor.matmul(dst[:], w[w_part][:, k, m * P:m * P + P], x[:, k, :],
                                                  start=(k == 0 and i == 0),
                                                  stop=(k == KH - 1 and i == len(products) - 1))
                    mm.then_inc(front_ready, 1)

                def a_v(a, t):
                    dst = front_bank(a, f"v{t}")
                    if is_first(a):
                        pe.wait_ge(loaded, LOADED)
                        pe.wait_ge(wvb_split, 1)
                    pe.wait_ge(x_low_ready, a.at(1, 1))
                    for k in range(KH):
                        for i, (x, w_part) in enumerate(((xT_high, 0), (xT_high, 1), (xT_low, 0))):
                            mm = nc.tensor.matmul(dst[:, 0:D + H], x[:, k, t * P:t * P + P], wvb[w_part][:, k, :],
                                                  start=(k == 0 and i == 0), stop=(k == KH - 1 and i == 2))
                    mm.then_inc(front_ready, 1)

                def a_norm(a, m):
                    dst = front_bank(a, f"n{m}")
                    if is_first(a):
                        pe.wait_ge(headmask_ready, 1)
                    pe.wait_ge(qsq_low_ready, a.at(KH, m + 1))
                    for i in range(2):
                        mm = nc.tensor.matmul(dst[:], headmask_r[:], qsq_part[i][:],
                                              start=(i == 0), stop=(i == 1))
                    mm.then_inc(front_ready, 1)

                def a_k(n, a, t):
                    dst = front_bank(a, f"t{t}")
                    if n and t < 2:
                        pe.wait_ge(x_out, n.at(KH, t + 1))
                    pe.wait_ge(front_out, a.at(NFA, FRONT_ACT.index("k1") + 1))
                    for m in range(KH):
                        mm = nc.tensor.transpose(dst[:, m * P:m * P + P], kT[:, m, t * P:t * P + P],
                                                 ident[:])
                    mm.then_inc(front_ready, 1)

                def b_scores(b, t, u):
                    if t == 0 and u == 0:
                        pe.wait_ge(stack_landed[b.parity], b.at_half(STACK_INCS, STACK_INCS))
                    wait_for(pe, masked, b.at(T * UNITS, UNITS * t + u - 1))
                    for i in range(UH):
                        m, head = divmod(u * UH + i, HM)
                        mm = nc.tensor.matmul(score[u % 2][:, i, :], ks[b.parity][:, head, m, t * P:t * P + P],
                                              qs[b.parity][:, head, m, t * P:t * P + P], start=True, stop=True)
                    mm.then_inc(scored, 1)

                def b_heads(b, t):
                    pe.wait_ge(vz_ready, b.at(T, t + 1))
                    pe.wait_ge(masked, b.at(T * UNITS, UNITS * (t + 1)))
                    wait_for(pe, attn_ready, b.at(T, t))
                    if t:
                        pe.wait_ge(state_ready, b.at(T - 1, t))
                    for m in range(KH):
                        if t:
                            nc.tensor.matmul(oT[:, m, :], state[:, m, :], qT[b.parity][:, m, t * P:t * P + P],
                                             start=True, stop=False, skip_group_check=True)
                        for odd in range(2):
                            for g in range(4):
                                head = 2 * g + odd
                                mm = nc.tensor.matmul(
                                    oT[32 * g:32 * g + 32, m, :],
                                    vz[b.parity][:, t, 4 * m + g, DH * odd:DH * odd + 2 * DH],
                                    probs[:, 2 * m + head // UH, head % UH, :],
                                    start=(t == 0 and odd == 0), stop=(odd == 1), skip_group_check=True)
                    mm.then_inc(oT_ready, 1)

                def b_state(b, t):
                    wait_for(pe, state_ready, b.at(T - 1, t))
                    for m in range(KH):
                        mm = nc.tensor.matmul(kv[:, m, :], ktok[:, t, m * P:m * P + P],
                                              v_heads(vz[b.parity], t, 4 * m, 4),
                                              start=(t == 0 and m == 0), stop=(t == T - 2),
                                              skip_group_check=True)
                    mm.then_inc(kv_ready, 1)

                def b_project(b, t):
                    pe.wait_ge(attn_ready, b.at(T, t + 1))
                    if t == 0:
                        wait_for(pe, out_ready, b.at(T, -T))
                    else:
                        pe.wait_ge(h2_ready, b.at(T, t))
                    for m in range(KH):
                        mm = nc.tensor.matmul(tok[:], attnT[t % 2][:, m, :], wo[:, m, :],
                                              start=(m == 0), stop=(m == KH - 1))
                    mm.then_inc(wo_ready, 1)

                def c_y(b, c, k):
                    if k == 0 and b:
                        wait_for(pe, out_ready, c.at(T, 0))
                    elif k == 0:
                        pe.wait_ge(cps_out, c.at(3, 0))
                    elif b:
                        pe.wait_ge(cps_out, c.at(3, 1))
                    for t in range(T):
                        if t < T // 2:
                            pe.wait_ge(yn_ready, c.at(T // 2, t + 1))
                        else:
                            pe.wait_ge(yn_ready_act, c.at(T // 2, t + 1 - T // 2))
                        mm = nc.tensor.transpose(y_bank(b, k)[:, t * P:t * P + P], yn[:, t, k * P:k * P + P], ident[:])
                    mm.then_inc(cps_ready, 1)

                def c_lowrank(c, tiles):
                    pe.wait_ge(cps_out, c.at(3, 2))
                    for t in tiles:
                        for k in range(KH):
                            mm = nc.tensor.matmul(cps[:, t * NR:t * NR + NR], yT[:, k, t * P:t * P + P], war[:, k, :],
                                                  start=(k == 0), stop=(k == KH - 1))
                    if t == T - 1:
                        mm.then_inc(cps_ready, 1)

                def c_turn(c):
                    pe.wait_ge(gating, c.at(GATE_STEPS, GATE_STEPS))
                    for t in range(T):
                        mm = nc.tensor.transpose(cps[0:BR, t * P:t * P + P], aw[:, t, :], ident[:])
                    mm.then_inc(cps_ready, 1)

                def c_base(a, b, c, t):
                    shared = b and not a
                    if a and t == 1:
                        pe.wait_ge(h2_ready, b.at(T, T))
                    elif a and t:
                        pe.wait_ge(out_ready, c.at(T, t - 1))
                    elif shared and t == 0:
                        pe.wait_ge(front_out, b.at(NFA, NFA))
                    for k in range(KH):
                        nc.tensor.matmul(ffn_bank(a, b, t), yT[:, k, t * P:t * P + P], wbase[:, k, :],
                                         start=(k == 0 and not (shared and t % 2)), stop=False,
                                         skip_group_check=bool(shared))

                def c_low(a, b, c, t):
                    pe.wait_ge(cps_out, c.at(3, 3))
                    nc.tensor.matmul(ffn_bank(a, b, t), awT[:, t * P:t * P + P], wb[:], start=False, stop=True,
                                     skip_group_check=bool(b and not a)).then_inc(ffn_ready, 1)

                def c_ffn(a, b, c, t):
                    if t % 2 == 0:
                        pe.wait_ge(cps_out, c.at(3, 3))
                    c_base(a, b, c, t)
                    c_low(a, b, c, t)

                def run_draining(b, c):
                    b_scores(b, 1, 0)
                    b_scores(b, 1, 1)
                    b_heads(b, 0)
                    b_state(b, 0)
                    c_y(b, c, 0)
                    b_scores(b, 1, 2)
                    c_y(b, c, 1)
                    b_scores(b, 1, 3)
                    b_scores(b, 2, 0)
                    c_lowrank(c, (0, 1))
                    b_heads(b, 1)
                    b_state(b, 1)
                    b_scores(b, 2, 1)
                    c_lowrank(c, (2, 3))
                    b_project(b, 0)
                    b_scores(b, 2, 2)
                    c_base(None, b, c, 0)
                    b_scores(b, 2, 3)
                    b_scores(b, 3, 0)
                    c_base(None, b, c, 1)
                    b_heads(b, 2)
                    b_state(b, 2)
                    b_scores(b, 3, 1)
                    b_project(b, 1)
                    b_scores(b, 3, 2)
                    c_base(None, b, c, 2)
                    b_scores(b, 3, 3)
                    b_project(b, 2)
                    b_heads(b, 3)
                    b_project(b, 3)
                    c_turn(c)
                    c_base(None, b, c, 3)
                    for t in range(T):
                        c_low(None, b, c, t)

                def run_last(c):
                    c_y(None, c, 0)
                    c_y(None, c, 1)
                    c_lowrank(c, range(T))
                    pe.wait_ge(out_ready, c.at(T, 0))
                    for t in range(T):
                        c_base(None, None, c, t)
                    c_turn(c)
                    for t in range(T):
                        c_low(None, None, c, t)

                def run(n, a, b, c):
                    if b and not a:
                        return run_draining(b, c)
                    if c and not b:
                        return run_last(c)
                    if a:
                        a_qk(a, "q", wq, 0)
                        a_qk(a, "q", wq, 1)
                    if b and is_first(b):
                        a_qk(a, "k", wk, 0)
                        b_scores(b, 0, 0)
                        b_scores(b, 0, 1)
                        a_qk(a, "k", wk, 1)
                        b_scores(b, 0, 2)
                        b_scores(b, 0, 3)
                    if b:
                        b_heads(b, 0)
                        b_scores(b, 1, 0)
                    if a and not (b and is_first(b)):
                        a_qk(a, "k", wk, 0)
                    if b:
                        b_scores(b, 1, 1)
                        b_state(b, 0)
                    if c:
                        c_y(b, c, 0)
                    if a and not (b and is_first(b)):
                        a_qk(a, "k", wk, 1)
                    if b:
                        b_scores(b, 1, 2)
                    if c:
                        c_y(b, c, 1)
                    if b:
                        b_scores(b, 1, 3)
                    if a:
                        a_v(a, 0)

                    if c:
                        c_lowrank(c, (0,))
                    if b:
                        b_heads(b, 1)
                        b_state(b, 1)
                        b_scores(b, 2, 0)
                    if c:
                        c_lowrank(c, (1,))
                    if b:
                        b_scores(b, 2, 1)
                    if c:
                        c_lowrank(c, (2, 3))
                    if b:
                        b_scores(b, 2, 2)
                        b_project(b, 0)
                    if a:
                        a_v(a, 1)
                    if b:
                        b_scores(b, 2, 3)
                    if a:
                        a_norm(a, 0)
                        a_v(a, 2)

                    if b:
                        b_heads(b, 2)
                        b_state(b, 2)
                        b_scores(b, 3, 0)
                    if b:
                        b_scores(b, 3, 1)
                        b_project(b, 1)
                    if b:
                        b_scores(b, 3, 2)
                    if a:
                        a_v(a, 3)
                    if b:
                        b_scores(b, 3, 3)
                    if a and is_first(a):
                        n_x(n, a, 0)
                        a_norm(a, 1)
                    elif a:
                        a_norm(a, 1)
                    if n and not (a and is_first(a)):
                        n_x(n, a, 0)

                    if b:
                        b_heads(b, 3)
                        b_project(b, 2)
                    if a:
                        a_k(n, a, 0)
                    if n:
                        n_x(n, a, 1)
                    if c:
                        c_turn(c)
                    if b:
                        b_project(b, 3)
                    if a:
                        a_k(n, a, 1)
                        a_k(n, a, 2)
                    if a and b:
                        b_scores(a, 0, 0)
                    if c:
                        c_ffn(a, b, c, 0)
                    if a and b:
                        b_scores(a, 0, 1)
                    if a:
                        a_k(n, a, 3)
                    if c:
                        c_ffn(a, b, c, 1)
                    if a and b:
                        b_scores(a, 0, 2)
                    if c:
                        c_ffn(a, b, c, 2)
                    if a and b:
                        b_scores(a, 0, 3)
                    if c:
                        c_ffn(a, b, c, 3)

                steps(pe, run)


def kernel(x, L0_tok_weight, L0_tok_bias, L0_attn_Wq, L0_attn_Wk, L0_attn_Wv, L0_attn_Wo, L0_attn_Wb,
           L0_attn_bb, L0_ffn_base_W, L0_ffn_base_b, L0_ffn_shared_A, L0_ffn_shared_B, L0_ffn_routed_A,
           L0_ffn_routed_B, L0_ffn_router_W, L0_ffn_router_b):
    import concourse.bacc as bacc
    from concourse.bass_utils import run_bass_kernel_spmd

    def row(v):
        return np.asarray(v).reshape(-1)

    def by_dimension(w):
        return np.asarray(w).reshape(D, KH, HM, DH).transpose(0, 1, 3, 2).reshape(D, D)

    base_b = np.asarray(L0_ffn_base_b)[None, :]
    i, j = np.arange(E)[:, None], np.arange(E)[None, :]
    head = np.arange(P) // DH
    arrays = {
        "tokens": np.asarray(x).reshape(SEQS * T, P).T,
        "table": np.asarray(L0_tok_weight).T,
        "tok_bias": row(L0_tok_bias),
        "w_q": by_dimension(L0_attn_Wq),
        "w_k": by_dimension(L0_attn_Wk),
        "w_vb": np.concatenate([np.asarray(L0_attn_Wv), np.asarray(L0_attn_Wb)], axis=1),
        "bb": row(L0_attn_bb),
        "w_o": np.asarray(L0_attn_Wo),
        "w_base": np.asarray(L0_ffn_base_W).T,
        "w_ar": np.concatenate([np.asarray(L0_ffn_routed_A).reshape(E * R, D), np.asarray(L0_ffn_shared_A),
                                np.asarray(L0_ffn_router_W)], axis=0).T,
        "w_b": np.concatenate([np.asarray(L0_ffn_routed_B).transpose(0, 2, 1).reshape(E * R, D),
                               np.asarray(L0_ffn_shared_B).T, base_b], axis=0),
        "router_b": row(L0_ffn_router_b),
        "ident": np.eye(P, dtype=np.float32),
        "causal": np.triu(np.ones((P, P), np.float32)),
        "headmask": (np.arange(P)[:, None] % HM == head[None, :]).astype(np.float32),
        "order": np.stack([j > i, j < i], axis=1).astype(np.float32).reshape(-1),
    }
    arrays = {name + "_in": np.ascontiguousarray(a) for name, a in arrays.items()}

    nc = bacc.Bacc("TRN2", target_bir_lowering=False, num_devices=1)
    args = [nc.dram_tensor(name, a.shape, U32 if name == "tokens_in" else mybir.dt.from_np(a.dtype),
                           kind="ExternalInput").ap() for name, a in arrays.items()]
    result = nc.dram_tensor("result", (SEQS * L, D), F32, kind="ExternalOutput").ap()
    scratch = nc.dram_tensor("scratch", (2, 2, PARTS, P, KH * L), BF16, kind="Internal").ap()
    build(nc, *args, scratch, result)
    r = run_bass_kernel_spmd(nc, [arrays], core_ids=[0])
    return r.results[0]["result"].reshape(SEQS, L, D)
```
